# Optimizing a Trainium2 kernel written in Bass

```python
import numpy as np
import jax
import jax.numpy as jnp

def _softmax(x, axis=-1):
    return jax.nn.softmax(x, axis=axis)

def _gelu(x):
    return jax.nn.gelu(x, approximate=True)

def _silu(x):
    return jax.nn.silu(x)

def _sigmoid(x):
    return jax.nn.sigmoid(x)

def _layernorm(x, axis=-1, eps=1e-05):
    m = jnp.mean(x, axis=axis, keepdims=True)
    v = jnp.var(x, axis=axis, keepdims=True)
    return (x - m) / jnp.sqrt(v + eps)

def _scatter_add(tgt, idx, src, axis=0):
    return tgt.at[idx].add(src)

def _segment_sum(src, seg, n):
    return jax.ops.segment_sum(src, seg, n)
kernel_name = 'mk_adj_resnorm_d2_adj_r2_5267ed'

def setup_inputs(seed: int=0):
    np.random.seed(seed)
    _w = jnp.asarray

    def _rec_inputs():
        import jax
        import jax.numpy as jnp
        _gk = jax.random.key(seed)
        x = 7.22e-05 + 1 * jax.random.normal(jax.random.fold_in(_gk, 1), (32, 256, 256), jnp.float32)
        _w = (1.0 + jnp.arange(256, dtype=jnp.float32)) ** (-0.5)
        _w = _w / _w.mean()
        _pij = jnp.clip(0.0078125 * _w[:, None] * _w[None, :], 0.0, 1.0)
        _a = jax.random.uniform(jax.random.fold_in(_gk, 2), (256, 256)) < _pij
        _a = jnp.logical_or(_a, jnp.swapaxes(_a, -1, -2))
        _a = jnp.logical_or(_a, jnp.eye(256, dtype=bool))
        _af = _a.astype(jnp.float32)
        _af = _af * jax.random.uniform(jax.random.fold_in(_gk, 3), (256, 256), jnp.float32, 0.05, 0.00390622)
        adj = _af
        return (x, adj)
    x, adj = _rec_inputs()

    def _L0_gnn_setup():
        import jax, jax.numpy as jnp
        import numpy as np
        B, N, D, T = (64, 128, 256, 3)

        def _lin(v, W, b):
            return jnp.einsum('...i,oi->...o', v, W) + b
        key = jax.random.key(seed)
        ks = jax.random.split(key, 12)
        s2 = 1.0 / np.sqrt(2 * D)
        s1 = 1.0 / np.sqrt(D)
        return {'x': jax.random.normal(ks[0], (B, N, D), jnp.float32), 'in_mat': jax.random.uniform(ks[1], (N, N), jnp.float32) / N, 'out_mat': jax.random.uniform(ks[2], (N, N), jnp.float32) / N, 'w3_w': jax.random.normal(ks[3], (D, 2 * D), jnp.float32) * s2, 'w3_b': jnp.zeros((D,), jnp.float32), 'u3_w': jax.random.normal(ks[4], (D, D), jnp.float32) * s1, 'u3_b': jnp.zeros((D,), jnp.float32), 'w4_w': jax.random.normal(ks[5], (D, 2 * D), jnp.float32) * s2, 'w4_b': jnp.zeros((D,), jnp.float32), 'w5_w': jax.random.normal(ks[6], (D, 2 * D), jnp.float32) * s2, 'w5_b': jnp.zeros((D,), jnp.float32), 'u5_w': jax.random.normal(ks[7], (D, D), jnp.float32) * s1, 'u5_b': jnp.zeros((D,), jnp.float32)}
    _L0_gnn_all = _L0_gnn_setup()
    _L0_gnn_in = {k: v for k, v in _L0_gnn_all.items() if k in ('w3_w', 'w3_b', 'u3_w', 'u3_b', 'w4_w', 'w4_b', 'w5_w', 'w5_b', 'u5_w', 'u5_b')}
    del _L0_gnn_all

    def _L1_gnn_setup():
        import jax, jax.numpy as jnp
        import numpy as np
        B, N, D, H = (4, 1024, 256, 8)
        HD = D // H
        key = jax.random.key(seed)
        ks = jax.random.split(key, 10)
        x = jax.random.normal(ks[0], (B, N, D), dtype=jnp.float32)
        adj = (jax.random.uniform(ks[1], (N, N)) < 0.1).astype(jnp.float32)
        s = 1.0 / np.sqrt(D)
        Wq = jax.random.normal(ks[2], (D, D), dtype=jnp.float32) * s
        Wk = jax.random.normal(ks[3], (D, D), dtype=jnp.float32) * s
        Wv = jax.random.normal(ks[4], (D, D), dtype=jnp.float32) * s
        Wo = jax.random.normal(ks[5], (D, D), dtype=jnp.float32) * s
        bq = jnp.zeros((D,), jnp.float32)
        bk = jnp.zeros((D,), jnp.float32)
        bv = jnp.zeros((D,), jnp.float32)
        bo = jnp.zeros((D,), jnp.float32)
        return {'x': x, 'adj': adj, 'Wq': Wq, 'bq': bq, 'Wk': Wk, 'bk': bk, 'Wv': Wv, 'bv': bv, 'Wo': Wo, 'bo': bo}
    _L1_gnn_all = _L1_gnn_setup()
    _L1_gnn_in = {k: v for k, v in _L1_gnn_all.items() if k in ('Wq', 'bq', 'Wk', 'bk', 'Wv', 'bv', 'Wo', 'bo')}
    del _L1_gnn_all
    return {'x': x, 'adj': adj, 'L0_gnn_w3_w': _L0_gnn_in['w3_w'], 'L0_gnn_w3_b': _L0_gnn_in['w3_b'], 'L0_gnn_u3_w': _L0_gnn_in['u3_w'], 'L0_gnn_u3_b': _L0_gnn_in['u3_b'], 'L0_gnn_w4_w': _L0_gnn_in['w4_w'], 'L0_gnn_w4_b': _L0_gnn_in['w4_b'], 'L0_gnn_w5_w': _L0_gnn_in['w5_w'], 'L0_gnn_w5_b': _L0_gnn_in['w5_b'], 'L0_gnn_u5_w': _L0_gnn_in['u5_w'], 'L0_gnn_u5_b': _L0_gnn_in['u5_b'], 'L1_gnn_Wq': _L1_gnn_in['Wq'], 'L1_gnn_bq': _L1_gnn_in['bq'], 'L1_gnn_Wk': _L1_gnn_in['Wk'], 'L1_gnn_bk': _L1_gnn_in['bk'], 'L1_gnn_Wv': _L1_gnn_in['Wv'], 'L1_gnn_bv': _L1_gnn_in['bv'], 'L1_gnn_Wo': _L1_gnn_in['Wo'], 'L1_gnn_bo': _L1_gnn_in['bo']}

def reference(x, adj, L0_gnn_w3_w, L0_gnn_w3_b, L0_gnn_u3_w, L0_gnn_u3_b, L0_gnn_w4_w, L0_gnn_w4_b, L0_gnn_w5_w, L0_gnn_w5_b, L0_gnn_u5_w, L0_gnn_u5_b, L1_gnn_Wq, L1_gnn_bq, L1_gnn_Wk, L1_gnn_bk, L1_gnn_Wv, L1_gnn_bv, L1_gnn_Wo, L1_gnn_bo):
    import jax
    import jax.numpy as jnp

    def _L0_gnn_ref(x, in_mat, out_mat, w3_w, w3_b, u3_w, u3_b, w4_w, w4_b, w5_w, w5_b, u5_w, u5_b):
        import jax, jax.numpy as jnp
        import numpy as np
        B, N, D, T = (64, 128, 256, 3)

        def _lin(v, W, b):
            return jnp.einsum('...i,oi->...o', v, W) + b
        h = x
        for _ in range(T):
            a_in = jnp.einsum('nm,bmd->bnd', in_mat, h)
            a_out = jnp.einsum('nm,bmd->bnd', out_mat, h)
            av = jnp.concatenate([a_in, a_out], axis=-1)
            z = jax.nn.sigmoid(_lin(av, w3_w, w3_b) + _lin(h, u3_w, u3_b))
            r = jax.nn.sigmoid(_lin(av, w4_w, w4_b) + _lin(h, u3_w, u3_b))
            hv = jnp.tanh(_lin(av, w5_w, w5_b) + _lin(r * h, u5_w, u5_b))
            h = (1.0 - z) * h + z * hv
        return h

    def _L1_gnn_ref(x, adj, Wq, bq, Wk, bk, Wv, bv, Wo, bo):
        import jax, jax.numpy as jnp
        import numpy as np
        B, N, D, H = (4, 1024, 256, 8)
        HD = D // H
        b, n, d = x.shape
        q = (x @ Wq + bq).reshape(b, n, H, HD)
        k = (x @ Wk + bk).reshape(b, n, H, HD)
        v = (x @ Wv + bv).reshape(b, n, H, HD)
        scores = jnp.einsum('bqhd,bkhd->bhqk', q, k) / jnp.sqrt(jnp.float32(HD))
        scores = scores + (1.0 - adj)[None, None, :, :] * -1000000000.0
        attn = jax.nn.softmax(scores, axis=-1)
        out = jnp.einsum('bhqk,bkhd->bqhd', attn, v).reshape(b, n, d)
        return out @ Wo + bo
    x = _layernorm(x + _L0_gnn_ref(x, adj, adj, L0_gnn_w3_w, L0_gnn_w3_b, L0_gnn_u3_w, L0_gnn_u3_b, L0_gnn_w4_w, L0_gnn_w4_b, L0_gnn_w5_w, L0_gnn_w5_b, L0_gnn_u5_w, L0_gnn_u5_b), axis=-1)
    x = _layernorm(x + _L1_gnn_ref(x, adj, L1_gnn_Wq, L1_gnn_bq, L1_gnn_Wk, L1_gnn_bk, L1_gnn_Wv, L1_gnn_bv, L1_gnn_Wo, L1_gnn_bo), axis=-1)
    return x

_drawn_inputs = setup_inputs


def setup_inputs(seed=0):
    import zlib

    import numpy as np

    out = dict(_drawn_inputs(seed))
    spreads = {'L0_gnn_w3_b': (0.0, 0.464),
     'L0_gnn_u3_b': (0.0, 0.408),
     'L0_gnn_w4_b': (0.0, 0.8),
     'L0_gnn_w5_b': (0.0, 0.1),
     'L0_gnn_u5_b': (0.0, 0.1),
     'L1_gnn_bq': (0.0, 0.1),
     'L1_gnn_bk': (0.0, 0.1),
     'L1_gnn_bv': (0.0, 0.1),
     'L1_gnn_bo': (0.0, 0.1)}
    factors = {'L0_gnn_w3_w': 3.816, 'L0_gnn_w4_w': 8.0}
    for name, (base, spread) in spreads.items():
        noise = np.random.default_rng([zlib.crc32(name.encode()), seed]).standard_normal(out[name].shape)
        drawn = base * np.exp(spread * noise) if base else spread * noise
        out[name] = jnp.asarray(drawn.astype(out[name].dtype))
    for name, factor in factors.items():
        out[name] = (out[name] * factor).astype(out[name].dtype)
    return out
```

```python
from contextlib import ExitStack

import concourse.bass as bass
from concourse import mybir

P = 128
BATCHES, N, D, STEPS = 32, 256, 256, 3
HEADS = 8
HEAD_DIM = D // HEADS
PAIR = 2
PAIRS = BATCHES // PAIR
C = D // P
HEADS_PER_CHUNK = P // HEAD_DIM
EPS = 1e-5
SMALL = 10
MASK = 1e9
SCORE_SCALE = float(HEAD_DIM) ** -0.5
PROJECT, FIRST_HEAD = 1, 2
LAST_HEAD = FIRST_HEAD + HEADS - 1
BATCH_SLOTS = FIRST_HEAD + HEADS
SUMS, SPREAD, OUTPUT, NORM = BATCH_SLOTS + 1, BATCH_SLOTS + 2, BATCH_SLOTS + 3, BATCH_SLOTS + 4
ATTENTION_SLOTS = BATCH_SLOTS + NORM
STAGES = (("u", 1), ("a", 1), ("r", 1), ("z", 1), ("v", 1), ("w", 2), ("t", 1))


def nth(i, per_iteration, k):
    return i * per_iteration + (k + 1)


def lately(i, per_iteration, k):
    return nth(i, per_iteration, max(k, -1))


def from_one(count):
    return count + 1


def build(nc, x, xT, adj, adjT, w3T, w3b, u3T, u3b, w4T, w4b, w5T, w5b, u5T, u5b,
          wq, bq, wk, bk, wv, bv, wo, bo, out):
    f32, f32r = mybir.dt.float32, mybir.dt.float32r
    ALU, ACT = mybir.AluOpType, mybir.ActivationFunctionType
    G = STEPS * C
    H = PAIR * HEADS
    TILE = C * PAIR * D

    ctx = ExitStack()
    with ctx:
        def sb(name, shape, dt=f32):
            return ctx.enter_context(nc.sbuf_tensor(name, shape, dt))

        def split_pair(name, shape):
            return sb(name + "_hi", shape, f32r), sb(name + "_lo", shape, f32r)

        def sem(name):
            return ctx.enter_context(nc.semaphore(name))

        def bank(name):
            return ctx.enter_context(nc.psum_tensor(name, [P, 512], f32))

        stage = [sb(f"stage{n}", [P, 2 * C, D]) for n in range(3)]
        adjT_s = split_pair("adjT", [P, C, N])
        w_s = {n: split_pair(n, [P, C, D]) for n in ("w3", "w4", "w5", "u3", "u5", "wq", "wk", "wv", "wo")}
        mask = sb("mask", [P, C, N])
        ident = sb("ident", [P, P])
        power = sb("power", [P, 4])
        raw_bias = sb("raw_bias", [P, 7, C])
        bias_r, bias_z, bias_v = sb("bias_r", [P, C]), sb("bias_z", [P, C]), sb("bias_v", [P, C])
        bias_q = sb("bias_q", [P, C])
        bv_rows, bo_rows = sb("bv_rows", [P, D]), sb("bo_rows", [P, D])
        x_in, xT_in = sb("x_in", [P, C, PAIR, D]), sb("xT_in", [P, C, PAIR, N])
        x_res = sb("x_res", [P, C, PAIR, D])
        h_hi, h_lo = split_pair("h", [P, C, PAIR, D])
        hT = sb("hT", [P, C, PAIR * N])
        hT_hi, hT_lo = split_pair("hT", [P, C, PAIR * N])
        aT_hi, aT_lo = split_pair("aT", [P, C, PAIR * N])
        uT = sb("uT", [P, C, PAIR * N])
        r_pre, z_pre = sb("r_pre", [P, C, PAIR * N]), sb("z_pre", [P, C, PAIR * N])
        r_tanh, z_tanh = sb("r_tanh", [P, C, PAIR * N]), sb("z_tanh", [P, C, PAIR * N])
        rhT = sb("rhT", [P, C, PAIR * N])
        rhT_hi, rhT_lo = split_pair("rhT", [P, C, PAIR * N])
        cand = sb("cand", [P, C, PAIR * N])
        move = sb("move", [P, C, PAIR * N])
        gate_move = sb("gate_move", [P, C, PAIR * N])
        y1 = sb("y1", [P, C, PAIR, D])
        x1 = sb("x1", [P, C, PAIR, D])
        stats1, mv1, var1, rstd1 = (sb("stats1", [P, 4, 6]), sb("mv1", [P, 4, 2]), sb("var1", [P, 4]),
                                    sb("rstd1", [P, 4]))
        x1_bo = [sb(f"x1_bo{b}", [P, C, D]) for b in range(PAIR)]
        y2 = [sb(f"y2_{b}", [P, C, D]) for b in range(PAIR)]
        stats2 = [sb(f"stats2_{b}", [P, C, 6]) for b in range(PAIR)]
        mv2 = [sb(f"mv2_{b}", [P, C, 2]) for b in range(PAIR)]
        var2 = [sb(f"var2_{b}", [P, C]) for b in range(PAIR)]
        rstd2 = [sb(f"rstd2_{b}", [P, C]) for b in range(PAIR)]
        out_sb = [sb(f"out_sb{b}", [P, C, D]) for b in range(PAIR)]
        x1T_hi, x1T_lo = split_pair("x1T", [P, C, N])
        qT, kT = sb("qT", [P, C, N]), sb("kT", [P, C, N])
        qT_hi, qT_lo = split_pair("qT", [P, C, N])
        kT_hi, kT_lo = split_pair("kT", [P, C, N])
        v_sb = sb("v_sb", [P, C, D])
        neg_scores = sb("neg_scores", [P, 2, C, N])
        neg_max = [sb(f"neg_max{b}", [P, HEADS, C]) for b in range(PAIR)]
        sums = [sb(f"sums{b}", [P, HEADS, C]) for b in range(PAIR)]
        inverse = [sb(f"inverse{b}", [P, HEADS, C]) for b in range(PAIR)]
        inverse_wide = sb("inverse_wide", [P, C, C, P])
        probs = sb("probs", [P, 2, C, N])
        probsT = sb("probsT", [P, 2, C, N])
        spread_sb = sb("spread_sb", [P, C, N])
        oT = sb("oT", [P, C, N])
        oT_hi, oT_lo = split_pair("oT", [P, C, N])

        gate_bank = [bank(f"gate_bank{n}") for n in range(4)]
        score_bank = [bank(f"score_bank{n}") for n in range(2)]
        turn_bank, mix_bank = bank("turn_bank"), bank("mix_bank")

        stage_loaded = [sem(f"stage_loaded{n}") for n in range(3)]
        small_loaded = sem("small_loaded")
        hi_made, lo_made, sum_made = sem("hi_made"), sem("lo_made"), sem("sum_made")
        ident_zero, ident_ready = sem("ident_zero"), sem("ident_ready")
        bias_step, bias_ready, mask_step = sem("bias_step"), sem("bias_ready"), sem("mask_step")
        x_loaded, x_kept = sem("x_loaded"), sem("x_kept")
        stored = [sem(f"stored{b}") for b in range(PAIR)]
        u_prod, a_prod, r_prod, z_prod, v_prod, h_turned = (
            sem("u_prod"), sem("a_prod"), sem("r_prod"), sem("z_prod"), sem("v_prod"), sem("h_turned"))
        u_copied, a_hi_made, a_lo_made = sem("u_copied"), sem("a_hi_made"), sem("a_lo_made")
        r_summed, r_tanh_made, rh_made = sem("r_summed"), sem("r_tanh_made"), sem("rh_made")
        rh_hi_made, rh_lo_made = sem("rh_hi_made"), sem("rh_lo_made")
        z_summed, z_tanh_made = sem("z_summed"), sem("z_tanh_made")
        cand_made, move_made, gate_move_made, h_new = (
            sem("cand_made"), sem("move_made"), sem("gate_move_made"), sem("h_new"))
        hT_hi_made, hT_lo_made, h_hi_made, h_lo_made = (
            sem("hT_hi_made"), sem("hT_lo_made"), sem("h_hi_made"), sem("h_lo_made"))
        y1_made, stats1_made, mv1_made, var1_made, rstd1_made, x1_made = (
            sem("y1_made"), sem("stats1_made"), sem("mv1_made"), sem("var1_made"), sem("rstd1_made"),
            sem("x1_made"))
        x1_turned, q_prod, k_prod, vv_prod = sem("x1_turned"), sem("q_prod"), sem("k_prod"), sem("vv_prod")
        scored, probs_turned, mixed, spread, o_prod = (
            sem("scored"), sem("probs_turned"), sem("mixed"), sem("spread"), sem("o_prod"))
        x1T_hi_made, x1T_lo_made = sem("x1T_hi_made"), sem("x1T_lo_made")
        q_made, k_made, v_made = sem("q_made"), sem("k_made"), sem("v_made")
        q_hi_made, k_hi_made, q_split, k_split = (
            sem("q_hi_made"), sem("k_hi_made"), sem("q_split"), sem("k_split"))
        masked, probs_made, probsT_made = sem("masked"), sem("probs_made"), sem("probsT_made")
        inverse_made, inverse_wide_made, spread_copied = (
            sem("inverse_made"), sem("inverse_wide_made"), sem("spread_copied"))
        oT_made, oT_hi_made, oT_lo_made = sem("oT_made"), sem("oT_hi_made"), sem("oT_lo_made")
        x1_bo_made, y2_made, stats2_made, mv2_made, var2_made, rstd2_made, out_made = (
            sem("x1_bo_made"), sem("y2_made"), sem("stats2_made"), sem("mv2_made"), sem("var2_made"),
            sem("rstd2_made"), sem("out_made"))

        def flat(t):
            return t[:].rearrange("p c n -> p (c n)")

        def wait_ge(engine, semaphore, value):
            if not isinstance(value, int) or value > 0:
                engine.wait_ge(semaphore, value)

        def stand_alone(engine):
            engine.nop(nofuse=True)

        def attention_pieces(slot):
            return [(b, slot - b * BATCH_SLOTS) for b in range(PAIR)
                    if 0 <= slot - b * BATCH_SLOTS <= NORM]

        def schedule():
            slot = 0
            for s in range(STEPS):
                for stage_name, follow in STAGES:
                    yield "gated", stage_name, s
                    for _ in range(follow):
                        yield "attention", slot, None
                        slot += 1
            while slot <= ATTENTION_SLOTS:
                yield "attention", slot, None
                slot += 1

        def iterations(engine, body):
            body(0, None)
            with engine.Fori(0, PAIRS - 1) as j:
                body(j + 1, j)
            body(None, PAIRS - 1)

        prepared = [(adjT, adjT_s, C), (w3T, w_s["w3"], 2 * C), (w4T, w_s["w4"], 2 * C),
                    (w5T, w_s["w5"], 2 * C), (u3T, w_s["u3"], C), (u5T, w_s["u5"], C),
                    (wq, w_s["wq"], C), (wk, w_s["wk"], C), (wv, w_s["wv"], C), (wo, w_s["wo"], C)]
        CHANGED = (1, 2, 3, 5)

        block = ctx.enter_context(nc.Block())

        @block.sync
        def _(sp):
            def load_pair(i):
                for b in range(PAIR):
                    at = bass.ds(i * PAIR + b, 1)
                    sp.dma_start(x_in[:, :, b, :],
                                 x[at].rearrange("b (c p) d -> p (b c) d", p=P)).then_inc(x_loaded, 16)
                    sp.dma_start(xT_in[:, :, b, :],
                                 xT[at].rearrange("b (c p) n -> p (b c) n", p=P)).then_inc(x_loaded, 16)

            for made in stored:
                sp.nop().then_inc(made, 16)
            for n, bias in enumerate((w3b, w4b, w5b, u3b, u5b, bq, bk)):
                sp.dma_start(raw_bias[:, n, :], bias).then_inc(small_loaded, 16)
            sp.dma_start(bv_rows[:], bv.partition_broadcast(P)).then_inc(small_loaded, 16)
            sp.dma_start(bo_rows[:], bo.partition_broadcast(P)).then_inc(small_loaded, 16)
            sp.dma_start(mask[:], adj.rearrange("(c p) n -> p c n", p=P)).then_inc(small_loaded, 16)
            load_pair(0)
            for n, (src, _, chunks) in enumerate(prepared):
                if n >= 3:
                    sp.wait_ge(lo_made, n - 2)
                sp.dma_start(stage[n % 3][:, 0:chunks, :],
                             src.rearrange("(c p) n -> p c n", p=P)).then_inc(stage_loaded[n % 3], 16)

            def store(j, b):
                sp.wait_ge(out_made, nth(j, PAIR, b))
                stand_alone(sp)
                sp.dma_start(out[bass.ds(j * PAIR + b, 1)].rearrange("b (c p) d -> p (b c) d", p=P),
                             out_sb[b][:]).then_inc(stored[b], 16)

            def next_pair(i):
                sp.wait_ge(h_lo_made, nth(i - 1, G, C - 1))
                sp.wait_ge(hT_lo_made, nth(i - 1, G, C - 1))
                sp.wait_ge(h_new, nth(i - 1, G, C - 1))
                stand_alone(sp)
                sp.wait_ge(x_kept, nth(i - 1, 1, 0))
                stand_alone(sp)
                load_pair(i)

            next_pair(1)
            with sp.Fori(0, PAIRS - 2) as j:
                next_pair(j + 2)
                for b in range(PAIR):
                    store(j, b)
            for j in (PAIRS - 2, PAIRS - 1):
                for b in range(PAIR):
                    store(j, b)
            for b in range(PAIR):
                sp.wait_ge(stored[b], from_one(PAIRS) * 16)

        @block.tensor
        def _(pe):
            def product(psum, left, right, left_at, right_at):
                passes = [(l, r, c) for c in range(C) for l, r in ((0, 0), (0, 1), (1, 0))]
                for n, (l, r, c) in enumerate(passes):
                    last = nc.tensor.matmul(psum, left_at(left[l], c), right_at(right[r], c),
                                            start=(n == 0), stop=(n == len(passes) - 1))
                return last

            def columns(k):
                return lambda t, c: t[:, c, k * P:(k + 1) * P]

            def whole(t, c):
                return t[:, c, :]

            def gated(stage_name, s, i):
                if stage_name == "u":
                    for c in range(C):
                        pe.wait_ge(hT_hi_made, nth(i, G, C * s + 1))
                        pe.wait_ge(hT_lo_made, nth(i, G, C * s + 1))
                        wait_ge(pe, cand_made, lately(i, G, C * (s - 1) + c))
                        product(gate_bank[c][:], w_s["u3"], (hT_hi, hT_lo), columns(c),
                                whole).then_inc(u_prod, 1)
                if stage_name == "a":
                    pe.wait_ge(h_hi_made, nth(i, G, C * s + 1))
                    pe.wait_ge(h_lo_made, nth(i, G, C * s + 1))
                    if s == 0:
                        wait_ge(pe, y1_made, nth(i, C, -1))
                    for c in range(C):
                        for b in range(PAIR):
                            last = product(gate_bank[2 + c][:, b * N:(b + 1) * N], (h_hi, h_lo), adjT_s,
                                           lambda t, k, b=b, c=c: t[:, k, b, c * P:(c + 1) * P], whole)
                        last.then_inc(a_prod, 1)
                if stage_name == "r":
                    for c in range(C):
                        pe.wait_ge(a_hi_made, nth(i, G, C * s + 1))
                        pe.wait_ge(a_lo_made, nth(i, G, C * s + 1))
                        pe.wait_ge(u_copied, nth(i, G, C * s + c))
                        product(gate_bank[c][:], w_s["w4"], (aT_hi, aT_lo), columns(c),
                                whole).then_inc(r_prod, 1)
                if stage_name == "z":
                    for c in range(C):
                        product(gate_bank[2 + c][:], w_s["w3"], (aT_hi, aT_lo), columns(c),
                                whole).then_inc(z_prod, 1)
                if stage_name in "vw":
                    left, right = ((w_s["w5"], (aT_hi, aT_lo)) if stage_name == "v"
                                   else (w_s["u5"], (rhT_hi, rhT_lo)))
                    for c in range(C):
                        if stage_name == "v":
                            pe.wait_ge(r_summed, nth(i, G, C * s + c))
                        else:
                            pe.wait_ge(rh_hi_made, nth(i, G, C * s + 1))
                            pe.wait_ge(rh_lo_made, nth(i, G, C * s + 1))
                        passes = [(l, r, k) for k in range(C) for l, r in ((0, 0), (0, 1), (1, 0))]
                        for n, (l, r, k) in enumerate(passes):
                            last = nc.tensor.matmul(
                                gate_bank[c][:], left[l][:, k, c * P:(c + 1) * P], right[r][:, k, :],
                                start=(stage_name == "v" and n == 0),
                                stop=(stage_name == "w" and n == len(passes) - 1), skip_group_check=True)
                        if stage_name == "w":
                            last.then_inc(v_prod, 1)
                if stage_name == "t":
                    pe.wait_ge(z_summed, nth(i, G, C * s + 1))
                    for n in range(C):
                        for c in range(C):
                            pe.wait_ge(h_new, nth(i, G, C * s + c))
                            for b in range(PAIR):
                                last = nc.tensor.matmul(
                                    gate_bank[2 + n][:, b * D + c * P:b * D + (c + 1) * P],
                                    hT[:, c, b * N + n * P:b * N + (n + 1) * P], ident[:],
                                    is_transpose=True, start=True, stop=True)
                        last.then_inc(h_turned, 1)

            def attention(slot, j):
                for b, piece in attention_pieces(slot):
                    if piece == 0:
                        pe.wait_ge(x1_made, nth(j, 1, 0))
                        wait_ge(pe, masked, from_one(nth(j, H, HEADS * b - 1)))
                        for c in range(C):
                            for n in range(C):
                                last = nc.tensor.matmul(
                                    score_bank[0][:, c * N + n * P:c * N + (n + 1) * P],
                                    x1[:, n, b, c * P:(c + 1) * P], ident[:],
                                    is_transpose=True, start=True, stop=True)
                        last.then_inc(x1_turned, 1)
                    if piece == PROJECT:
                        pe.wait_ge(x1T_hi_made, nth(j, PAIR, b))
                        pe.wait_ge(x1T_lo_made, nth(j, PAIR, b))
                        for c in range(C):
                            last = product(score_bank[1][:, c * N:(c + 1) * N], w_s["wq"],
                                           (x1T_hi, x1T_lo), columns(c), whole)
                        last.then_inc(q_prod, 1)
                        wait_ge(pe, probsT_made, from_one(nth(j, H, HEADS * b - 1)))
                        for c in range(C):
                            last = product(turn_bank[:, c * N:(c + 1) * N], w_s["wk"],
                                           (x1T_hi, x1T_lo), columns(c), whole)
                        last.then_inc(k_prod, 1)
                        for n in range(C):
                            last = product(score_bank[0][:, n * D:(n + 1) * D], (x1T_hi, x1T_lo),
                                           w_s["wv"], columns(n), whole)
                        last.then_inc(vv_prod, 1)
                    if FIRST_HEAD <= piece <= LAST_HEAD:
                        h = piece - FIRST_HEAD
                        c, r = divmod(h, HEADS_PER_CHUNK)
                        rows = slice(r * HEAD_DIM, (r + 1) * HEAD_DIM)
                        if h == 0:
                            pe.wait_ge(q_split, nth(j, PAIR, b))
                            pe.wait_ge(k_split, nth(j, PAIR, b))
                            pe.wait_ge(v_made, nth(j, PAIR, b))
                        if h >= 2:
                            pe.wait_ge(masked, from_one(nth(j, H, HEADS * b + h - 2)))
                        for n in range(C):
                            for m, (q, k) in enumerate(((qT_hi, kT_hi), (qT_hi, kT_lo), (qT_lo, kT_hi))):
                                last = nc.tensor.matmul(
                                    score_bank[h % 2][:, n * N:(n + 1) * N], q[rows, c, n * P:(n + 1) * P],
                                    k[rows, c, :], start=(m == 0), stop=(m == 2))
                        last.then_inc(scored, 1)
                    h = piece - FIRST_HEAD - 1
                    if 0 <= h < HEADS:
                        pe.wait_ge(probs_made, from_one(nth(j, H, HEADS * b + h)))
                        if h == 0:
                            pe.wait_ge(k_made, nth(j, PAIR, b))
                            wait_ge(pe, spread_copied, from_one(nth(j, PAIR, b - 1)))
                        else:
                            pe.wait_ge(probsT_made, from_one(nth(j, H, HEADS * b + h - 1)))
                        for n in range(C):
                            for m in range(C):
                                last = nc.tensor.matmul(
                                    turn_bank[:, m * N + n * P:m * N + (n + 1) * P],
                                    probs[:, h % 2, n, m * P:(m + 1) * P], ident[:],
                                    is_transpose=True, start=True, stop=True)
                        last.then_inc(probs_turned, 1)
                    h = piece - FIRST_HEAD - 2
                    if 0 <= h < HEADS:
                        c, r = divmod(h, HEADS_PER_CHUNK)
                        pe.wait_ge(probsT_made, from_one(nth(j, H, HEADS * b + h)))
                        if h == 0:
                            wait_ge(pe, y2_made, from_one(nth(j, PAIR, b - 1)))
                        for m in range(C):
                            last = nc.tensor.matmul(
                                mix_bank[r * HEAD_DIM:(r + 1) * HEAD_DIM, c * N:(c + 1) * N],
                                v_sb[:, m, h * HEAD_DIM:(h + 1) * HEAD_DIM], probsT[:, h % 2, m, :],
                                start=(m == 0), stop=(m == C - 1))
                        last.then_inc(mixed, 1)
                    if piece == SPREAD:
                        pe.wait_ge(inverse_wide_made, nth(j, PAIR, b))
                        pe.wait_ge(probsT_made, from_one(nth(j, H, HEADS * b + HEADS - 1)))
                        if b + 1 < PAIR:
                            pe.wait_ge(k_made, nth(j, PAIR, b + 1))
                        for c in range(C):
                            for n in range(C):
                                last = nc.tensor.matmul(
                                    turn_bank[:, c * N + n * P:c * N + (n + 1) * P],
                                    inverse_wide[:, n, c, :], ident[:], is_transpose=True,
                                    start=True, stop=True)
                        last.then_inc(spread, 1)
                    if piece == OUTPUT:
                        pe.wait_ge(oT_hi_made, nth(j, PAIR, b))
                        pe.wait_ge(oT_lo_made, nth(j, PAIR, b))
                        for n in range(C):
                            last = product(mix_bank[:, n * D:(n + 1) * D], (oT_hi, oT_lo), w_s["wo"],
                                           columns(n), whole)
                        last.then_inc(o_prod, 1)

            def body(i, j):
                for kind, what, s in schedule():
                    if kind == "gated" and i is not None:
                        gated(what, s, i)
                    if kind == "attention" and j is not None:
                        attention(what, j)

            nc.tensor.nop().then_inc(mixed, 1)
            pe.wait_ge(lo_made, len(prepared))
            pe.wait_ge(hi_made, len(prepared))
            pe.wait_ge(ident_ready, 1)
            iterations(pe, body)

        @block.scalar
        def _(act):
            for made in (probs_made, probsT_made, spread_copied):
                nc.scalar.nop().then_inc(made, 1)
            for n, (_, parts, _) in enumerate(prepared):
                if n in CHANGED:
                    act.wait_ge(sum_made, CHANGED.index(n) + 1)
                else:
                    act.wait_ge(stage_loaded[n % 3], 16 * (n // 3 + 1))
                nc.scalar.activation(flat(parts[0]), stage[n % 3][:, 0:C, :].rearrange("p c n -> p (c n)"),
                                     ACT.Identity).then_inc(hi_made, 1)
            act.wait_ge(bias_ready, 1)

            def gated(stage_name, s, i):
                def k(c):
                    return nth(i, G, C * s + c)

                if stage_name == "u":
                    if s == 0:
                        act.wait_ge(x_loaded, nth(i, 2 * PAIR, 2 * PAIR - 1) * 16)
                        wait_ge(act, v_prod, nth(i, G, -1))
                        for c in range(C):
                            nc.scalar.activation(hT_hi[:, c, :], xT_in[:, c].rearrange("p b n -> p (b n)"),
                                                 ACT.Identity).then_inc(hT_hi_made, 1)
                        for c in range(C):
                            nc.scalar.activation(h_hi[:, c].rearrange("p b n -> p (b n)"),
                                                 x_in[:, c].rearrange("p b n -> p (b n)"),
                                                 ACT.Identity).then_inc(h_hi_made, 1)
                    wait_ge(act, z_summed, nth(i, G, C * s - 1))
                    for c in range(C):
                        act.wait_ge(u_prod, k(c))
                        nc.scalar.activation(uT[:, c, :], gate_bank[c][:], ACT.Identity).then_inc(u_copied, 1)
                if stage_name == "a":
                    for c in range(C):
                        act.wait_ge(a_prod, k(c))
                        nc.scalar.activation(aT_hi[:, c, :], gate_bank[2 + c][:],
                                             ACT.Identity).then_inc(a_hi_made, 1)
                if stage_name == "r":
                    for c in range(C):
                        act.wait_ge(r_summed, k(c))
                        nc.scalar.activation(r_tanh[:, c, :], r_pre[:, c, :], ACT.Tanh,
                                             bias=bias_r[:, c:c + 1], scale=0.5).then_inc(r_tanh_made, 1)
                if stage_name == "z":
                    for c in range(C):
                        act.wait_ge(rh_made, k(c))
                        nc.scalar.activation(rhT_hi[:, c, :], rhT[:, c, :], ACT.Identity).then_inc(rh_hi_made, 1)
                if stage_name == "v":
                    for c in range(C):
                        act.wait_ge(z_summed, k(c))
                        nc.scalar.activation(z_tanh[:, c, :], z_pre[:, c, :], ACT.Tanh,
                                             bias=bias_z[:, c:c + 1], scale=0.5).then_inc(z_tanh_made, 1)
                if stage_name == "w":
                    for c in range(C):
                        act.wait_ge(v_prod, k(c))
                        nc.scalar.activation(cand[:, c, :], gate_bank[c][:], ACT.Tanh,
                                             bias=bias_v[:, c:c + 1]).then_inc(cand_made, 1)
                if stage_name == "t" and s < STEPS - 1:
                    for c in range(C):
                        act.wait_ge(h_new, k(c))
                        nc.scalar.activation(hT_hi[:, c, :], hT[:, c, :], ACT.Identity).then_inc(hT_hi_made, 1)
                    for n in range(C):
                        act.wait_ge(h_turned, k(n))
                        nc.scalar.activation(h_hi[:, n].rearrange("p b n -> p (b n)"), gate_bank[2 + n][:],
                                             ACT.Identity).then_inc(h_hi_made, 1)

            def attention(slot, j):
                for b, piece in attention_pieces(slot):
                    if piece == 0:
                        act.wait_ge(x1_turned, nth(j, PAIR, b))
                        nc.scalar.activation(flat(x1T_hi), score_bank[0][:], ACT.Identity).then_inc(x1T_hi_made, 1)
                    if piece == PROJECT:
                        act.wait_ge(q_prod, nth(j, PAIR, b))
                        for c in range(C):
                            last = nc.scalar.activation(qT[:, c, :], score_bank[1][:, c * N:(c + 1) * N],
                                                        ACT.Identity, bias=bias_q[:, c:c + 1],
                                                        scale=-SCORE_SCALE)
                        last.then_inc(q_made, 1)
                        act.wait_ge(k_prod, nth(j, PAIR, b))
                        for c in range(C):
                            last = nc.scalar.activation(kT[:, c, :], turn_bank[:, c * N:(c + 1) * N],
                                                        ACT.Identity, bias=raw_bias[:, 6, c:c + 1])
                        last.then_inc(k_made, 1)
                    h = piece - FIRST_HEAD - 1
                    if 0 <= h < HEADS:
                        act.wait_ge(probs_turned, nth(j, H, HEADS * b + h))
                        wait_ge(act, mixed, from_one(lately(j, H, HEADS * b + h - 2)))
                        nc.scalar.activation(probsT[:, h % 2].rearrange("p c n -> p (c n)"), turn_bank[:],
                                             ACT.Identity).then_inc(probsT_made, 1)
                    h = piece - FIRST_HEAD
                    if 0 <= h < HEADS:
                        act.wait_ge(masked, from_one(nth(j, H, HEADS * b + h)))
                        for n in range(C):
                            last = nc.scalar.activation(
                                probs[:, h % 2, n, :], neg_scores[:, h % 2, n, :], ACT.Exp, scale=-1.0,
                                bias=neg_max[b][:, h, n:n + 1], accum_out=sums[b][:, h, n:n + 1])
                        last.then_inc(probs_made, 1)
                    if piece == SPREAD:
                        act.wait_ge(spread, nth(j, PAIR, b))
                        nc.scalar.activation(flat(spread_sb), turn_bank[:], ACT.Identity).then_inc(spread_copied, 1)
                        act.wait_ge(oT_made, nth(j, PAIR, b))
                        nc.scalar.activation(flat(oT_hi), flat(oT), ACT.Identity).then_inc(oT_hi_made, 1)

            def body(i, j):
                for kind, what, s in schedule():
                    if kind == "gated" and i is not None:
                        gated(what, s, i)
                    if kind == "attention" and j is not None:
                        attention(what, j)

            iterations(act, body)

        @block.vector
        def _(dve):
            for made in (masked, y2_made):
                nc.vector.nop().then_inc(made, 1)
            dve.wait_ge(small_loaded, 16 * SMALL)
            nc.vector.tensor_tensor(bias_r[:], raw_bias[:, 1, :], raw_bias[:, 3, :], ALU.add)
            nc.vector.tensor_tensor(bias_z[:], raw_bias[:, 0, :], raw_bias[:, 3, :], ALU.add)
            nc.vector.tensor_tensor(bias_v[:], raw_bias[:, 2, :], raw_bias[:, 4, :], ALU.add)
            nc.vector.memset(power[:], -0.5)
            nc.vector.tensor_scalar(flat(mask), flat(mask), -1.0, 1.0, ALU.mult, ALU.add).then_inc(bias_step, 1)
            dve.wait_ge(bias_step, 1)
            nc.vector.tensor_scalar(flat(mask), flat(mask), MASK, None, ALU.mult)
            nc.vector.tensor_scalar(bias_r[:], bias_r[:], 0.5, None, ALU.mult)
            nc.vector.tensor_scalar(bias_z[:], bias_z[:], 0.5, None, ALU.mult)
            nc.vector.tensor_scalar(bias_q[:], raw_bias[:, 5, :], -SCORE_SCALE, None,
                                    ALU.mult).then_inc(bias_ready, 1)
            for n, (_, parts, chunks) in enumerate(prepared):
                st = stage[n % 3]
                first = st[:, 0:C, :].rearrange("p c n -> p (c n)")
                if n in CHANGED:
                    dve.wait_ge(stage_loaded[n % 3], 16 * (n // 3 + 1))
                    if chunks > C:
                        nc.vector.tensor_tensor(first, first, st[:, C:2 * C, :].rearrange("p c n -> p (c n)"),
                                                ALU.add).then_inc(sum_made, 1)
                    else:
                        nc.vector.tensor_scalar(first, first, 0.5, None, ALU.mult).then_inc(sum_made, 1)
                dve.wait_ge(hi_made, n + 1)
                nc.vector.tensor_tensor(flat(parts[1]), first, flat(parts[0]).bitcast(f32),
                                        ALU.subtract).then_inc(lo_made, 1)

            def rest(lo, full, hi, done):
                nc.vector.tensor_tensor(lo, full, hi.bitcast(f32), ALU.subtract).then_inc(done, 1)

            def gated(stage_name, s, i):
                def k(c):
                    return nth(i, G, C * s + c)

                def h_old(c):
                    return hT[:, c, :] if s else xT_in[:, c].rearrange("p b n -> p (b n)")

                if stage_name == "u" and s == 0:
                    for c in range(C):
                        dve.wait_ge(hT_hi_made, k(c))
                        rest(hT_lo[:, c, :], h_old(c), hT_hi[:, c, :], hT_lo_made)
                    for c in range(C):
                        dve.wait_ge(h_hi_made, k(c))
                        rest(h_lo[:, c].rearrange("p b n -> p (b n)"),
                             x_in[:, c].rearrange("p b n -> p (b n)"),
                             h_hi[:, c].rearrange("p b n -> p (b n)"), h_lo_made)
                if stage_name == "a":
                    for c in range(C):
                        dve.wait_ge(a_hi_made, k(c))
                        rest(aT_lo[:, c, :], gate_bank[2 + c][:], aT_hi[:, c, :], a_lo_made)
                if stage_name == "r":
                    for c in range(C):
                        dve.wait_ge(r_prod, k(c))
                        dve.wait_ge(u_copied, k(c))
                        nc.vector.tensor_tensor(r_pre[:, c, :], gate_bank[c][:], uT[:, c, :],
                                                ALU.add).then_inc(r_summed, 1)
                if stage_name == "z":
                    for c in range(C):
                        dve.wait_ge(r_tanh_made, k(c))
                        nc.vector.scalar_tensor_tensor(out=rhT[:, c, :], in0=r_tanh[:, c, :], scalar=1.0,
                                                       in1=h_old(c), op0=ALU.add,
                                                       op1=ALU.mult).then_inc(rh_made, 1)
                    for c in range(C):
                        dve.wait_ge(z_prod, k(c))
                        nc.vector.tensor_tensor(z_pre[:, c, :], gate_bank[2 + c][:], uT[:, c, :],
                                                ALU.add).then_inc(z_summed, 1)
                    for c in range(C):
                        dve.wait_ge(rh_hi_made, k(c))
                        rest(rhT_lo[:, c, :], rhT[:, c, :], rhT_hi[:, c, :], rh_lo_made)
                if stage_name == "w":
                    for c in range(C):
                        dve.wait_ge(cand_made, k(c))
                        nc.vector.tensor_tensor(move[:, c, :], cand[:, c, :], h_old(c),
                                                ALU.subtract).then_inc(move_made, 1)
                    for c in range(C):
                        dve.wait_ge(z_tanh_made, k(c))
                        dve.wait_ge(move_made, k(c))
                        nc.vector.scalar_tensor_tensor(out=gate_move[:, c, :], in0=z_tanh[:, c, :],
                                                       scalar=1.0, in1=move[:, c, :], op0=ALU.add,
                                                       op1=ALU.mult).then_inc(gate_move_made, 1)
                    for c in range(C):
                        dve.wait_ge(gate_move_made, k(c))
                        nc.vector.scalar_tensor_tensor(out=hT[:, c, :], in0=gate_move[:, c, :], scalar=0.5,
                                                       in1=h_old(c), op0=ALU.mult,
                                                       op1=ALU.add).then_inc(h_new, 1)
                if stage_name == "t" and s < STEPS - 1:
                    for c in range(C):
                        dve.wait_ge(hT_hi_made, nth(i, G, C * (s + 1) + c))
                        rest(hT_lo[:, c, :], hT[:, c, :], hT_hi[:, c, :], hT_lo_made)
                    for n in range(C):
                        dve.wait_ge(h_hi_made, nth(i, G, C * (s + 1) + n))
                        rest(h_lo[:, n].rearrange("p b n -> p (b n)"), gate_bank[2 + n][:],
                             h_hi[:, n].rearrange("p b n -> p (b n)"), h_lo_made)
                if stage_name == "t" and s == STEPS - 1:
                    for n in range(C):
                        dve.wait_ge(h_turned, k(n))
                        dve.wait_ge(x_kept, nth(i, 1, 0))
                        nc.vector.tensor_tensor(y1[:, n].rearrange("p b n -> p (b n)"), gate_bank[2 + n][:],
                                                x_res[:, n].rearrange("p b n -> p (b n)"),
                                                ALU.add).then_inc(y1_made, 1)
                    dve.wait_ge(y1_made, nth(i, C, C - 1))
                    for n in range(C):
                        for b in range(PAIR):
                            last = nc.vector.bn_stats(stats1[:, n * PAIR + b, :], y1[:, n, b, :])
                    last.then_inc(stats1_made, 1)
                    dve.wait_ge(stats1_made, nth(i, 1, 0))
                    stand_alone(dve)
                    for g in range(C * PAIR):
                        last = nc.vector.bn_aggr(mv1[:, g, :], stats1[:, g, :])
                    last.then_inc(mv1_made, 1)
                    dve.wait_ge(mv1_made, nth(i, 1, 0))
                    nc.vector.tensor_scalar(var1[:], mv1[:, :, 1], EPS, None, ALU.add).then_inc(var1_made, 1)
                    dve.wait_ge(rstd1_made, nth(i, 1, 0))
                    for n in range(C):
                        for b in range(PAIR):
                            g = n * PAIR + b
                            last = nc.vector.tensor_scalar(x1[:, n, b, :], y1[:, n, b, :], mv1[:, g, 0:1],
                                                           rstd1[:, g:g + 1], ALU.subtract, ALU.mult)
                    last.then_inc(x1_made, 1)

            def attention(slot, j):
                for b, piece in attention_pieces(slot):
                    def done(made):
                        dve.wait_ge(made, nth(j, PAIR, b))

                    if piece == 0:
                        done(x1T_hi_made)
                        rest(flat(x1T_lo), score_bank[0][:], flat(x1T_hi), x1T_lo_made)
                    if piece == PROJECT:
                        done(q_made)
                        nc.vector.tensor_copy(flat(qT_hi), flat(qT)).then_inc(q_hi_made, 1)
                        done(vv_prod)
                        nc.vector.tensor_tensor(v_sb[:], score_bank[0][:].rearrange("p (c n) -> p c n", c=C),
                                                bv_rows[:].unsqueeze(1).to_broadcast([P, C, D]),
                                                ALU.add).then_inc(v_made, 1)
                        done(k_made)
                        nc.vector.tensor_copy(flat(kT_hi), flat(kT)).then_inc(k_hi_made, 1)
                        done(q_hi_made)
                        rest(flat(qT_lo), flat(qT), flat(qT_hi), q_split)
                        done(k_hi_made)
                        rest(flat(kT_lo), flat(kT), flat(kT_hi), k_split)
                    h = piece - FIRST_HEAD
                    if 0 <= h < HEADS:
                        dve.wait_ge(scored, nth(j, H, HEADS * b + h))
                        wait_ge(dve, probs_made, from_one(lately(j, H, HEADS * b + h - 2)))
                        stand_alone(dve)
                        for n in range(C):
                            last = nc.vector.tensor_tensor_reduce(
                                out=neg_scores[:, h % 2, n, :], in0=score_bank[h % 2][:, n * N:(n + 1) * N],
                                in1=mask[:, n, :], scale=1.0, scalar=3.4e38, op0=ALU.add, op1=ALU.min,
                                accum_out=neg_max[b][:, h, n:n + 1])
                        last.then_inc(masked, 1)
                    if piece == SUMS:
                        dve.wait_ge(probs_made, from_one(nth(j, H, HEADS * b + HEADS - 1)))
                        nc.vector.reciprocal(inverse[b][:], sums[b][:]).then_inc(inverse_made, 1)
                        done(inverse_made)
                        for n in range(C):
                            last = nc.vector.tensor_copy(
                                inverse_wide[:, n].rearrange("p c (h d) -> p (c h) d", d=HEAD_DIM),
                                inverse[b][:, :, n:n + 1].to_broadcast([P, HEADS, HEAD_DIM]))
                        last.then_inc(inverse_wide_made, 1)
                    if piece == SPREAD:
                        dve.wait_ge(spread_copied, from_one(nth(j, PAIR, b)))
                        dve.wait_ge(mixed, from_one(nth(j, H, HEADS * b + HEADS - 1)))
                        nc.vector.tensor_tensor(flat(oT), mix_bank[:], flat(spread_sb),
                                                ALU.mult).then_inc(oT_made, 1)
                        done(oT_hi_made)
                        rest(flat(oT_lo), flat(oT), flat(oT_hi), oT_lo_made)
                    if piece == OUTPUT:
                        done(o_prod)
                        done(x1_bo_made)
                        nc.vector.tensor_tensor(flat(y2[b]), mix_bank[:], flat(x1_bo[b]),
                                                ALU.add).then_inc(y2_made, 1)
                        dve.wait_ge(y2_made, from_one(nth(j, PAIR, b)))
                        for n in range(C):
                            last = nc.vector.bn_stats(stats2[b][:, n, :], y2[b][:, n, :])
                        last.then_inc(stats2_made, 1)
                        done(stats2_made)
                        stand_alone(dve)
                        for n in range(C):
                            last = nc.vector.bn_aggr(mv2[b][:, n, :], stats2[b][:, n, :])
                        last.then_inc(mv2_made, 1)
                        done(mv2_made)
                        nc.vector.tensor_scalar(var2[b][:], mv2[b][:, :, 1], EPS, None,
                                                ALU.add).then_inc(var2_made, 1)
                    if piece == NORM:
                        done(rstd2_made)
                        dve.wait_ge(stored[b], from_one(j) * 16)
                        for n in range(C):
                            last = nc.vector.tensor_scalar(out_sb[b][:, n, :], y2[b][:, n, :],
                                                           mv2[b][:, n, 0:1], rstd2[b][:, n:n + 1],
                                                           ALU.subtract, ALU.mult)
                        last.then_inc(out_made, 1)

            def body(i, j):
                for kind, what, s in schedule():
                    if kind == "gated" and i is not None:
                        gated(what, s, i)
                    if kind == "attention" and j is not None:
                        attention(what, j)

            iterations(dve, body)

        @block.gpsimd
        def _(pool):
            nc.gpsimd.memset(ident[:], 0.0).then_inc(ident_zero, 1)
            pool.wait_ge(ident_zero, 1)
            nc.gpsimd.affine_select(out=ident[:], in_=ident[:], compare_op=ALU.not_equal, fill=1.0, base=0,
                                    pattern=[[-1, P]], channel_multiplier=1).then_inc(ident_ready, 1)
            pool.wait_ge(small_loaded, 16 * SMALL)
            pool.wait_ge(bias_ready, 1)

            def add_bo(j, b):
                pool.wait_ge(x1_made, nth(j, 1, 0))
                wait_ge(pool, y2_made, from_one(nth(j, PAIR, -1)))
                nc.gpsimd.tensor_tensor(x1_bo[b][:], x1[:, :, b, :],
                                        bo_rows[:].unsqueeze(1).to_broadcast([P, C, D]),
                                        ALU.add).then_inc(x1_bo_made, 1)

            def second_rstd(j, b):
                pool.wait_ge(var2_made, nth(j, PAIR, b))
                nc.gpsimd.tensor_tensor(rstd2[b][:], var2[b][:], power[:, 0:C], ALU.pow).then_inc(rstd2_made, 1)

            def body(i, j):
                if i is not None:
                    pool.wait_ge(x_loaded, nth(i, 2 * PAIR, 2 * PAIR - 1) * 16)
                    wait_ge(pool, y1_made, nth(i, C, -1))
                    stand_alone(pool)
                    nc.gpsimd.tensor_copy(x_res[:], x_in[:]).then_inc(x_kept, 1)
                if j is not None:
                    for b in range(PAIR):
                        add_bo(j, b)
                    second_rstd(j, 0)
                if i is not None:
                    pool.wait_ge(var1_made, nth(i, 1, 0))
                    nc.gpsimd.tensor_tensor(rstd1[:], var1[:], power[:], ALU.pow).then_inc(rstd1_made, 1)
                if j is not None:
                    second_rstd(j, 1)

            iterations(pool, body)


def kernel(**inputs):
    import numpy as np
    import concourse.bacc as bacc
    from concourse import mybir as mb
    from concourse.bass_utils import run_bass_kernel_spmd

    def turned(a):
        return np.ascontiguousarray(np.swapaxes(a, -1, -2))

    g0, g1 = "L0_gnn_", "L1_gnn_"
    arrays = {"x": inputs["x"], "xT": turned(inputs["x"]), "adj": inputs["adj"], "adjT": turned(inputs["adj"])}
    for n in ("w3", "u3", "w4", "w5", "u5"):
        arrays[n + "T"] = turned(inputs[f"{g0}{n}_w"])
        arrays[n + "b"] = inputs[f"{g0}{n}_b"]
    for n in "qkvo":
        arrays["w" + n] = inputs[f"{g1}W{n}"]
        arrays["b" + n] = inputs[f"{g1}b{n}"]
    for n in ("w3b", "w4b", "w5b", "u3b", "u5b", "bq", "bk"):
        arrays[n] = turned(arrays[n].reshape(C, P))
    arrays = {n: np.ascontiguousarray(a) for n, a in arrays.items()}

    nc = bacc.Bacc("TRN2", target_bir_lowering=False, num_devices=1)
    args = {n: nc.dram_tensor(n, a.shape, mb.dt.from_np(a.dtype), kind="ExternalInput").ap()
            for n, a in arrays.items()}
    out = nc.dram_tensor("out", arrays["x"].shape, mb.dt.float32, kind="ExternalOutput").ap()
    build(nc, out=out, **args)
    return run_bass_kernel_spmd(nc, [arrays], core_ids=[0]).results[0]["out"]
```

```python
from contextlib import ExitStack

import concourse.bass as bass
from concourse import mybir

P = 128
BATCHES, N, D, STEPS = 32, 256, 256, 3
HEADS = 8
HEAD_DIM = D // HEADS
PAIR = 2
PAIRS = BATCHES // PAIR
C = D // P
HEADS_PER_CHUNK = P // HEAD_DIM
EPS = 1e-5
SMALL = 10
MASK = 1e9
SCORE_SCALE = float(HEAD_DIM) ** -0.5
STEP = [(name, c) for name in "uarzvwt" for c in range(C)]
FOLLOW = [0, 1, 1, 0, 1, 0, 1, 0, 0, 0, 0, 1, 1, 2,
          2, 3, 2, 3, 0, 1, 1, 3, 0, 1, 0, 1, 2, 0,
          2, 1, 0, 2, 2, 3, 1, 2, 0, 2, 1, 2, 0, 0]
FIRST_STEPS = {(s, c) for s in range(STEPS - 1) for c in range(C)}
LAST_STEP = {(STEPS - 1, C - 1)}
TURNED = {(s, C - 1) for s in range(STEPS - 1)}
LAST_HEADS = {(b, HEADS - 1) for b in range(PAIR)}
SCALAR_ORDER = {
    "u_copy": ("u", 0.1), "a_hi": ("a", 0.1), "r_tanh": ("r", 0.8), "rh_hi": ("r", 3.2),
    "z_tanh": ("z", 2.6), "cand": ("w", 0.1), "hT_hi": ("w", 1.1, FIRST_STEPS),
    "h_hi": ("t", -0.8, TURNED), "split_x": ("v", 0.9, LAST_STEP),
    "x1T_hi": ("x1", -2.2), "q": ("q", -0.2), "k": ("k", -0.7), "v_hi": ("vv", 2.4),
    "exp": ("score", 0.4), "probsT_hi": ("turn", -1.8), "spread": ("spread", -0.9),
    "oT_hi": ("spread", 2.6)}
VECTOR_ORDER = {
    "a_lo": ("a", 0.6), "r_sum": ("r", 0), "rh": ("r", 1.3), "z_sum": ("z", -0.6),
    "gate": ("z", 2.6), "move": ("w", 0.1), "h_new": ("w", 1),
    "hT_lo": ("w", 2.3, FIRST_STEPS), "h_lo": ("t", 0.3, TURNED),
    "split_x": ("v", 3.5, LAST_STEP), "y1": ("t", 0.1, LAST_STEP), "norm1": ("t", 4.3, LAST_STEP),
    "x1T_lo": ("x1", -2), "q_lo": ("q", 0.6), "k_lo": ("k", 1), "v": ("vv", -1.5),
    "v_lo": ("vv", 2.6), "mask": ("score", 0), "probsT_lo": ("turn", -0.9),
    "inverse": ("score", 2.9, LAST_HEADS), "oT": ("spread", 0.9), "oT_lo": ("o", -1),
    "y2": ("o", -0.1), "norm2": ("o", 4.7)}
POOL_ORDER = {
    "keep_x": ("u", -0.7, {(0, 0)}), "rh_lo": ("r", 2.4), "keep": ("z", 2.3), "norm1": ("t", 3, LAST_STEP),
    "x1_bo": ("q", 0.6), "norm2": ("o", 2.3)}
DMA_ORDER = {
    "q_stack": ("q", 0.8), "k_stack": ("k", 6.9), "load": ("w", 4.1, {(0, C - 1)}), "store": ("o", 3.4)}
Q_PARTS, K_PARTS = ("hi", "hi", "lo"), ("hi", "lo", "hi")
STACK = len(Q_PARTS) * HEAD_DIM
WINDOW = P - HEAD_DIM


def nth(i, per_iteration, k):
    return i * per_iteration + (k + 1)


def lately(i, per_iteration, k):
    return nth(i, per_iteration, max(k, -1))


def from_one(count):
    return count + 1


def attention_groups():
    groups = []

    def heads(b):
        for h in range(HEADS):
            groups.append([("score", b, h)])
            if h:
                groups.append([("turn", b, h - 1)] + ([("mix", b, h - 2)] if h > 1 else []))

    last = HEADS - 1
    groups += [[("x1", 0, 0)], [("q", 0, 0)], [("k", 0, 0)], [("vv", 0, 0)]]
    heads(0)
    groups += [[("x1", 1, 0)], [("turn", 0, last), ("mix", 0, last - 1)], [("q", 1, 0)],
               [("mix", 0, last)], [("k", 1, 0)], [("spread", 0, 0)], [("vv", 1, 0)], [("o", 0, 0)]]
    heads(1)
    groups += [[("turn", 1, last), ("mix", 1, last - 1)], [("mix", 1, last)], [("spread", 1, 0)],
               [("o", 1, 0)]]
    return groups


def tensor_plan():
    groups, plan = attention_groups(), []
    for n, follow in enumerate(FOLLOW):
        s, at = divmod(n, len(STEP))
        name, c = STEP[at]
        plan.append((name, s, c))
        for _ in range(follow):
            plan += groups.pop(0) if groups else []
    for group in groups:
        plan += group
    return plan


def plan_after(kinds):
    plan = tensor_plan()
    placed = []
    for name, (step, lag, *only) in kinds.items():
        for at, (of, x, y) in enumerate(plan):
            if of == step and (not only or (x, y) in only[0]):
                behind = lag[x] if isinstance(lag, tuple) else lag
                placed.append((at + behind, len(placed), (name, x, y)))
    return [what for _, _, what in sorted(placed)]


def build(nc, x, xT, adj, adjT, w3T, w3b, u3T, u3b, w4T, w4b, w5T, w5b, u5T, u5b,
          wq, bq, wk, bk, wv, bv, wo, bo, out):
    f32, f32r = mybir.dt.float32, mybir.dt.float32r
    ALU, ACT = mybir.AluOpType, mybir.ActivationFunctionType
    G = STEPS * C
    H = PAIR * HEADS

    ctx = ExitStack()
    with ctx:
        def sb(name, shape, dt=f32):
            return ctx.enter_context(nc.sbuf_tensor(name, shape, dt))

        def parts(name, shape):
            return sb(name + "_hi", shape, f32r), sb(name + "_lo", shape, f32r)

        def sem(name):
            return ctx.enter_context(nc.semaphore(name))

        def bank(name):
            return ctx.enter_context(nc.psum_tensor(name, [P, 512], f32))

        stage = [sb(f"stage{n}", [P, 2 * C, D]) for n in range(3)]
        w_s = {n: parts(n, [P, C, D])
               for n in ("adjT", "w3", "w4", "w5", "u3", "u5", "wq", "wk", "wv", "wo")}
        mask = sb("mask", [P, C, N])
        ident = sb("ident", [P, P])
        power = sb("power", [P, C * PAIR])
        raw_bias = sb("raw_bias", [P, 7, C])
        bias_r, bias_z, bias_v = sb("bias_r", [P, C]), sb("bias_z", [P, C]), sb("bias_v", [P, C])
        bias_q = sb("bias_q", [P, C])
        bv_rows, bo_rows = sb("bv_rows", [P, D]), sb("bo_rows", [P, D])
        wide = [P, C, PAIR * N]
        x_in, xT_in = sb("x_in", wide), sb("xT_in", wide)
        h_hi, h_lo = parts("h", wide)
        hT = sb("hT", wide)
        hT_hi, hT_lo = parts("hT", wide)
        aT_hi, aT_lo = parts("aT", wide)
        uT = sb("uT", wide)
        r_tanh, z_tanh = sb("r_tanh", wide), sb("z_tanh", wide)
        rhT = sb("rhT", wide)
        rhT_hi, rhT_lo = parts("rhT", wide)
        gate, kept = r_tanh, sb("kept", wide)
        cand = sb("cand", wide)
        y1 = sb("y1", [P, C, PAIR, D])
        x1 = sb("x1", [P, C, PAIR, D])
        stats1, mv1 = sb("stats1", [P, C * PAIR, 6]), sb("mv1", [P, C * PAIR, 2])
        var1, rstd1 = sb("var1", [P, C * PAIR]), sb("rstd1", [P, C * PAIR])
        x1_bo = [sb(f"x1_bo{b}", [P, C, D]) for b in range(PAIR)]
        y2 = [sb(f"y2_{b}", [P, C, D]) for b in range(PAIR)]
        stats2 = [sb(f"stats2_{b}", [P, C, 6]) for b in range(PAIR)]
        mv2 = [sb(f"mv2_{b}", [P, C, 2]) for b in range(PAIR)]
        var2 = [sb(f"var2_{b}", [P, C]) for b in range(PAIR)]
        rstd2 = [sb(f"rstd2_{b}", [P, C]) for b in range(PAIR)]
        x1T_hi, x1T_lo = parts("x1T", [P, C, N])
        qT, kT = sb("qT", [P, C, N]), sb("kT", [P, C, N])
        qT_s, kT_s = parts("qT", [P, C, N]), parts("kT", [P, C, N])
        q_stack, k_stack = sb("q_stack", [STACK, C, HEADS_PER_CHUNK, N], f32r), sb(
            "k_stack", [STACK, C, HEADS_PER_CHUNK, N], f32r)
        v_sb = sb("v_sb", [P, C, D])
        v_s = parts("v", [P, C, C, HEADS_PER_CHUNK, P])
        neg_scores, probs = (stage[n][:].rearrange("p (a c) n -> p a c n", c=C) for n in range(2))
        spread_sb, oT = stage[2][:, 0:C, :], stage[2][:, C:2 * C, :]
        neg_max = [sb(f"neg_max{b}", [P, HEADS, C]) for b in range(PAIR)]
        sums = [sb(f"sums{b}", [P, HEADS, C]) for b in range(PAIR)]
        inverse = [sb(f"inverse{b}", [P, HEADS, C]) for b in range(PAIR)]
        inverse_wide = sb("inverse_wide", [P, C, HEADS, HEAD_DIM])
        probsT_s = parts("probsT", [P, 2, C, N])
        oT_hi, oT_lo = parts("oT", [P, C, N])

        gate_bank = [bank(f"gate_bank{n}") for n in range(4)]
        score_bank = [bank(f"score_bank{n}") for n in range(2)]
        turn_bank, mix_bank = bank("turn_bank"), bank("mix_bank")

        stage_loaded = [sem(f"stage_loaded{n}") for n in range(3)]
        small_loaded = sem("small_loaded")
        hi_ready, lo_ready, sum_ready = sem("hi_ready"), sem("lo_ready"), sem("sum_ready")
        ident_zero, ident_ready, pads_zero = sem("ident_zero"), sem("ident_ready"), sem("pads_zero")
        bias_step, bias_ready = sem("bias_step"), sem("bias_ready")
        x_loaded, x_kept = sem("x_loaded"), sem("x_kept")
        stored = [sem(f"stored{b}") for b in range(PAIR)]
        u_prod, a_prod, r_prod, z_prod, v_prod, h_turned = (
            sem("u_prod"), sem("a_prod"), sem("r_prod"), sem("z_prod"), sem("v_prod"), sem("h_turned"))
        u_copied, a_hi_made, a_lo_made = sem("u_copied"), sem("a_hi_made"), sem("a_lo_made")
        r_summed, r_tanh_made, rh_made = sem("r_summed"), sem("r_tanh_made"), sem("rh_made")
        rh_hi_made, rh_lo_made = sem("rh_hi_made"), sem("rh_lo_made")
        z_summed, z_tanh_made, gate_made = sem("z_summed"), sem("z_tanh_made"), sem("gate_made")
        keep_made, kept_made = sem("keep_made"), sem("kept_made")
        cand_made, move_made, h_new = sem("cand_made"), sem("move_made"), sem("h_new")
        hT_hi_made, hT_lo_made, h_hi_made, h_lo_made = (
            sem("hT_hi_made"), sem("hT_lo_made"), sem("h_hi_made"), sem("h_lo_made"))
        y1_made, stats1_made, mv1_made, var1_made, rstd1_made, x1_made = (
            sem("y1_made"), sem("stats1_made"), sem("mv1_made"), sem("var1_made"), sem("rstd1_made"),
            sem("x1_made"))
        x1_turned, q_prod, k_prod, v_out = sem("x1_turned"), sem("q_prod"), sem("k_prod"), sem("v_out")
        scored, probs_turned, mixed, spread, o_prod = (
            sem("scored"), sem("probs_turned"), sem("mixed"), sem("spread"), sem("o_prod"))
        x1T_hi_made, x1T_lo_made = sem("x1T_hi_made"), sem("x1T_lo_made")
        q_made, k_made, v_made = sem("q_made"), sem("k_made"), sem("v_made")
        q_hi_made, k_hi_made, q_lo_made, k_lo_made = (
            sem("q_hi_made"), sem("k_hi_made"), sem("q_lo_made"), sem("k_lo_made"))
        v_hi_made, v_lo_made = sem("v_hi_made"), sem("v_lo_made")
        q_stacked, k_stacked = sem("q_stacked"), sem("k_stacked")
        masked, probs_made = sem("masked"), sem("probs_made")
        probsT_hi_made, probsT_lo_made = sem("probsT_hi_made"), sem("probsT_lo_made")
        inverse_made, inverse_wide_made, spread_copied = (
            sem("inverse_made"), sem("inverse_wide_made"), sem("spread_copied"))
        oT_made, oT_hi_made, oT_lo_made = sem("oT_made"), sem("oT_hi_made"), sem("oT_lo_made")
        x1_bo_made, y2_made, stats2_made, mv2_made, var2_made, rstd2_made, out_made = (
            sem("x1_bo_made"), sem("y2_made"), sem("stats2_made"), sem("mv2_made"), sem("var2_made"),
            sem("rstd2_made"), sem("out_made"))

        def flat(t):
            return t[:, :, :].rearrange("p c n -> p (c n)")

        def wait_ge(engine, semaphore, value):
            if not isinstance(value, int) or value > 0:
                engine.wait_ge(semaphore, value)

        def stand_alone(engine):
            engine.nop(nofuse=True)

        def windows(v_part):
            return v_part[:].rearrange("p a c r w -> p (a c) r w")[:, :, :, WINDOW:P]

        def by_head(t):
            return t[:].rearrange("p a (c r d) -> p (a c) r d", r=HEADS_PER_CHUNK, d=HEAD_DIM)

        gated_weights = [(u3T, "u3", C), (adjT, "adjT", C), (w4T, "w4", 2 * C), (w3T, "w3", 2 * C),
                         (w5T, "w5", 2 * C), (u5T, "u5", C)]
        all_weights = gated_weights + [(wq, "wq", C), (wk, "wk", C), (wv, "wv", C), (wo, "wo", C)]
        order_of = {name: n for n, (_, name, _) in enumerate(all_weights)}
        CHANGED = ("w4", "w3", "w5", "u5")
        SETUP = range(len(gated_weights))
        LATER = range(len(gated_weights), len(all_weights))

        def iterations(engine, body, later=None):
            body(0, None)
            if later:
                later(LATER)
            with engine.Fori(0, PAIRS - 1) as j:
                body(j + 1, j)
            body(None, PAIRS - 1)

        block = ctx.enter_context(nc.Block())

        @block.sync
        def _(sp):
            def load_pair(i):
                for b in range(PAIR):
                    at = bass.ds(i * PAIR + b, 1)
                    sp.dma_start(xT_in[:, :, b * N:(b + 1) * N],
                                 xT[at].rearrange("b (c p) n -> p (b c) n", p=P)).then_inc(x_loaded, 16)
                    sp.dma_start(x_in[:, :, b * D:(b + 1) * D],
                                 x[at].rearrange("b (c p) d -> p (b c) d", p=P)).then_inc(x_loaded, 16)

            def free_input(i):
                sp.wait_ge(h_lo_made, nth(i, G, C - 1))
                sp.wait_ge(hT_lo_made, nth(i, G, C - 1))
                sp.wait_ge(h_new, nth(i, G, C - 1))
                stand_alone(sp)
                sp.wait_ge(x_kept, nth(i, 1, 0))
                stand_alone(sp)

            for made in stored:
                sp.nop().then_inc(made, 16)
            load_pair(0)
            for n, (src, _, chunks) in enumerate(all_weights):
                if n >= 3:
                    sp.wait_ge(lo_ready, n - 2)
                sp.dma_start(stage[n % 3][:, 0:chunks, :],
                             src.rearrange("(c p) n -> p c n", p=P)).then_inc(stage_loaded[n % 3], 16)
                if n == 2:
                    for m, bias in enumerate((w3b, w4b, w5b, u3b, u5b, bq, bk)):
                        sp.dma_start(raw_bias[:, m, :], bias).then_inc(small_loaded, 16)
                    sp.dma_start(bv_rows[:], bv.partition_broadcast(P)).then_inc(small_loaded, 16)
                    sp.dma_start(bo_rows[:], bo.partition_broadcast(P)).then_inc(small_loaded, 16)
                    sp.dma_start(mask[:], adj.rearrange("(c p) n -> p c n", p=P)).then_inc(small_loaded, 16)
                if n == len(gated_weights):
                    free_input(0)
                    load_pair(1)

            plan = plan_after(DMA_ORDER)

            def stack(dst, source, order, part, stacked):
                for p in [p for p, of in enumerate(order) if of == part]:
                    for r in range(HEADS_PER_CHUNK):
                        rows = slice(r * HEAD_DIM, (r + 1) * HEAD_DIM)
                        sp.dma_start(dst[p * HEAD_DIM:(p + 1) * HEAD_DIM, :, r, :].bitcast(f32),
                                     source[part == "lo"][rows, :, :].bitcast(f32)).then_inc(stacked, 16)

            def body(i, j, after=None):
                for name, b, _ in plan:
                    if name == "load" and i is not None:
                        free_input(i)
                        load_pair(after)
                    if j is None:
                        continue
                    if name == "q_stack":
                        sp.wait_ge(q_hi_made, nth(j, PAIR, b))
                        stack(q_stack, qT_s, Q_PARTS, "hi", q_stacked)
                        sp.wait_ge(q_lo_made, nth(j, PAIR, b))
                        stack(q_stack, qT_s, Q_PARTS, "lo", q_stacked)
                    if name == "k_stack":
                        sp.wait_ge(k_hi_made, nth(j, PAIR, b))
                        stack(k_stack, kT_s, K_PARTS, "hi", k_stacked)
                        sp.wait_ge(k_lo_made, nth(j, PAIR, b))
                        stack(k_stack, kT_s, K_PARTS, "lo", k_stacked)
                    if name == "store":
                        sp.wait_ge(out_made, nth(j, PAIR, b))
                        stand_alone(sp)
                        sp.dma_start(out[bass.ds(j * PAIR + b, 1)].rearrange("b (c p) d -> p (b c) d", p=P),
                                     y2[b][:]).then_inc(stored[b], 16)

            with sp.Fori(0, PAIRS - 2) as j:
                body(j + 1, j, j + 2)
            body(PAIRS - 1, PAIRS - 2, 0)
            body(None, PAIRS - 1)
            for b in range(PAIR):
                sp.wait_ge(stored[b], from_one(PAIRS) * 16)

        @block.tensor
        def _(pe):
            TERMS = ((0, 0), (0, 1), (1, 0))

            def product(psum, left, right, left_at, right_at, start=True, stop=True):
                passes = [(l, r, c) for c in range(C) for l, r in TERMS]
                for n, (l, r, c) in enumerate(passes):
                    last = nc.tensor.matmul(psum, left_at(left[l], c), right_at(right[r], c),
                                            start=(start and n == 0),
                                            stop=(stop and n == len(passes) - 1), skip_group_check=True)
                return last

            def columns(k):
                return lambda t, c: t[:, c, k * P:(k + 1) * P]

            def whole(t, c):
                return t[:, c, :]

            def weight(name, i, s, c):
                if isinstance(i, int) and s == 0 and c == 0:
                    pe.wait_ge(lo_ready, order_of[name] + 1)
                return w_s[name]

            def gated(name, s, c, i):
                both, one = nth(i, G, C * s + 1), nth(i, G, C * s + c)
                if name == "u":
                    pe.wait_ge(hT_hi_made, both)
                    pe.wait_ge(hT_lo_made, both)
                    wait_ge(pe, cand_made, lately(i, G, C * (s - 1) + c))
                    product(gate_bank[c][:], weight("u3", i, s, c), (hT_hi, hT_lo), columns(c),
                            whole).then_inc(u_prod, 1)
                if name == "a":
                    pe.wait_ge(h_hi_made, both)
                    pe.wait_ge(h_lo_made, both)
                    if s == 0:
                        wait_ge(pe, y1_made, nth(i, C, -1))
                    adj_s = weight("adjT", i, s, c)
                    for b in range(PAIR):
                        last = product(gate_bank[2 + c][:, b * N:(b + 1) * N], (h_hi, h_lo), adj_s,
                                       columns(b * C + c), whole)
                    last.then_inc(a_prod, 1)
                if name == "r":
                    pe.wait_ge(a_hi_made, both)
                    pe.wait_ge(a_lo_made, both)
                    pe.wait_ge(u_copied, one)
                    product(gate_bank[c][:], weight("w4", i, s, c), (aT_hi, aT_lo), columns(c),
                            whole).then_inc(r_prod, 1)
                if name == "z":
                    product(gate_bank[2 + c][:], weight("w3", i, s, c), (aT_hi, aT_lo), columns(c),
                            whole).then_inc(z_prod, 1)
                if name == "v":
                    pe.wait_ge(r_summed, one)
                    product(gate_bank[c][:], weight("w5", i, s, c), (aT_hi, aT_lo), columns(c), whole,
                            stop=False)
                if name == "w":
                    pe.wait_ge(rh_hi_made, both)
                    pe.wait_ge(rh_lo_made, both)
                    product(gate_bank[c][:], weight("u5", i, s, c), (rhT_hi, rhT_lo), columns(c), whole,
                            start=False).then_inc(v_prod, 1)
                if name == "t":
                    if c == 0:
                        pe.wait_ge(z_summed, both)
                    pe.wait_ge(h_new, one)
                    for n in range(C):
                        for b in range(PAIR):
                            last = nc.tensor.matmul(
                                gate_bank[2 + n][:, b * D + c * P:b * D + (c + 1) * P],
                                hT[:, c, b * N + n * P:b * N + (n + 1) * P], ident[:],
                                is_transpose=True, start=True, stop=True)
                    if c == C - 1:
                        last.then_inc(h_turned, 1)

            def attention(name, b, h, j):
                batch, head = nth(j, PAIR, b), nth(j, H, HEADS * b + h)
                c, r = divmod(h, HEADS_PER_CHUNK)
                before = from_one(nth(j, H, HEADS * b - 1))
                if name == "x1":
                    pe.wait_ge(x1_made, nth(j, 1, 0))
                    pe.wait_ge(masked, before)
                    for c in range(C):
                        for n in range(C):
                            last = nc.tensor.matmul(
                                score_bank[0][:, c * N + n * P:c * N + (n + 1) * P],
                                x1[:, n, b, c * P:(c + 1) * P], ident[:],
                                is_transpose=True, start=True, stop=True)
                    last.then_inc(x1_turned, 1)
                if name == "q":
                    pe.wait_ge(x1T_hi_made, batch)
                    pe.wait_ge(x1T_lo_made, batch)
                    for c in range(C):
                        last = product(score_bank[1][:, c * N:(c + 1) * N], w_s["wq"],
                                       (x1T_hi, x1T_lo), columns(c), whole)
                    last.then_inc(q_prod, 1)
                if name == "k":
                    pe.wait_ge(probsT_hi_made, before)
                    pe.wait_ge(probsT_lo_made, before)
                    for c in range(C):
                        last = product(turn_bank[:, c * N:(c + 1) * N], w_s["wk"],
                                       (x1T_hi, x1T_lo), columns(c), whole)
                    last.then_inc(k_prod, 1)
                if name == "vv":
                    for n in range(C):
                        last = product(score_bank[0][:, n * D:(n + 1) * D], (x1T_hi, x1T_lo),
                                       w_s["wv"], columns(n), whole)
                    last.then_inc(v_out, 1)
                if name == "score":
                    if h == 0:
                        pe.wait_ge(q_stacked, batch * 16 * len(Q_PARTS) * HEADS_PER_CHUNK)
                        pe.wait_ge(k_stacked, batch * 16 * len(K_PARTS) * HEADS_PER_CHUNK)
                        pe.wait_ge(v_made, batch)
                    if h >= 2:
                        pe.wait_ge(masked, from_one(nth(j, H, HEADS * b + h - 2)))
                    for n in range(C):
                        last = nc.tensor.matmul(
                            score_bank[h % 2][:, n * N:(n + 1) * N], q_stack[:, c, r, n * P:(n + 1) * P],
                            k_stack[:, c, r, :], start=True, stop=True)
                    last.then_inc(scored, 1)
                if name == "turn":
                    pe.wait_ge(probs_made, from_one(head))
                    if h == 0:
                        pe.wait_ge(k_made, batch)
                        pe.wait_ge(spread_copied, from_one(nth(j, PAIR, b - 1)))
                    else:
                        pe.wait_ge(probsT_hi_made, from_one(nth(j, H, HEADS * b + h - 1)))
                        pe.wait_ge(probsT_lo_made, from_one(nth(j, H, HEADS * b + h - 1)))
                    for n in range(C):
                        for m in range(C):
                            last = nc.tensor.matmul(
                                turn_bank[:, m * N + n * P:m * N + (n + 1) * P],
                                probs[:, h % 2, n, m * P:(m + 1) * P], ident[:],
                                is_transpose=True, start=True, stop=True)
                    last.then_inc(probs_turned, 1)
                if name == "mix":
                    pe.wait_ge(probsT_hi_made, from_one(head))
                    pe.wait_ge(probsT_lo_made, from_one(head))
                    if h == 0:
                        pe.wait_ge(v_lo_made, batch)
                        pe.wait_ge(y2_made, from_one(nth(j, PAIR, b - 1)))
                    window = slice(r * WINDOW + WINDOW, r * WINDOW + WINDOW + P)
                    last = product(mix_bank[:, c * N:(c + 1) * N], v_s, probsT_s,
                                   lambda t, a: t[:, a, c].rearrange("p r w -> p (r w)")[:, window],
                                   lambda t, a: t[:, h % 2, a, :], start=(r == 0),
                                   stop=(r == HEADS_PER_CHUNK - 1))
                    last.then_inc(mixed, 1)
                if name == "spread":
                    pe.wait_ge(inverse_wide_made, batch)
                    pe.wait_ge(probsT_hi_made, from_one(nth(j, H, HEADS * b + HEADS - 1)))
                    pe.wait_ge(probsT_lo_made, from_one(nth(j, H, HEADS * b + HEADS - 1)))
                    if b + 1 < PAIR:
                        pe.wait_ge(k_made, nth(j, PAIR, b + 1))
                    for c in range(C):
                        for n in range(C):
                            last = nc.tensor.matmul(
                                turn_bank[:, c * N + n * P:c * N + (n + 1) * P],
                                inverse_wide[:, n].rearrange("p h d -> p (h d)")[:, c * P:(c + 1) * P],
                                ident[:], is_transpose=True, start=True, stop=True)
                    last.then_inc(spread, 1)
                if name == "o":
                    pe.wait_ge(oT_hi_made, batch)
                    pe.wait_ge(oT_lo_made, batch)
                    for n in range(C):
                        last = product(mix_bank[:, n * D:(n + 1) * D], (oT_hi, oT_lo), w_s["wo"],
                                       columns(n), whole)
                    last.then_inc(o_prod, 1)

            plan = tensor_plan()

            def body(i, j):
                for name, a, b in plan:
                    if name in "uarzvwt":
                        if i is not None:
                            gated(name, a, b, i)
                    elif j is not None:
                        attention(name, a, b, j)

            def all_in(_):
                pe.wait_ge(lo_ready, len(all_weights))

            nc.tensor.nop().then_inc(mixed, 1)
            pe.wait_ge(ident_ready, 1)
            iterations(pe, body, all_in)

        @block.scalar
        def _(act):
            def copy(to, source, done):
                nc.scalar.activation(to, source, ACT.Identity).then_inc(done, 1)

            def split_x(i):
                act.wait_ge(x_loaded, nth(i, 2 * PAIR, 2 * PAIR - 1) * 16)
                wait_ge(act, a_prod, nth(i, G, -1))
                for c in range(C):
                    copy(hT_hi[:, c, :], xT_in[:, c, :], hT_hi_made)
                for c in range(C):
                    copy(h_hi[:, c, :], x_in[:, c, :], h_hi_made)

            def prepare(which):
                for n in which:
                    name = all_weights[n][1]
                    if name in CHANGED:
                        act.wait_ge(sum_ready, CHANGED.index(name) + 1)
                    else:
                        act.wait_ge(stage_loaded[n % 3], 16 * (n // 3 + 1))
                    copy(flat(w_s[name][0]), stage[n % 3][:, 0:C, :].rearrange("p c n -> p (c n)"), hi_ready)

            for made in (probs_made, probsT_hi_made, spread_copied):
                nc.scalar.nop().then_inc(made, 1)
            split_x(0)
            prepare(SETUP)
            act.wait_ge(bias_ready, 1)

            plan = plan_after(SCALAR_ORDER)

            def gated(name, s, c, i):
                one = nth(i, G, C * s + c)
                if name == "u_copy":
                    act.wait_ge(u_prod, one)
                    wait_ge(act, z_summed, lately(i, G, C * (s - 1) + c))
                    copy(uT[:, c, :], gate_bank[c][:], u_copied)
                if name == "a_hi":
                    act.wait_ge(a_prod, one)
                    copy(aT_hi[:, c, :], gate_bank[2 + c][:], a_hi_made)
                if name == "r_tanh":
                    act.wait_ge(r_summed, one)
                    nc.scalar.activation(r_tanh[:, c, :], r_tanh[:, c, :], ACT.Tanh,
                                         bias=bias_r[:, c:c + 1], scale=0.5).then_inc(r_tanh_made, 1)
                if name == "rh_hi":
                    act.wait_ge(rh_made, one)
                    copy(rhT_hi[:, c, :], rhT[:, c, :], rh_hi_made)
                if name == "z_tanh":
                    act.wait_ge(z_summed, one)
                    wait_ge(act, keep_made, lately(i, G, C * (s - 1) + c))
                    nc.scalar.activation(z_tanh[:, c, :], z_tanh[:, c, :], ACT.Tanh,
                                         bias=bias_z[:, c:c + 1], scale=0.5).then_inc(z_tanh_made, 1)
                if name == "cand":
                    act.wait_ge(v_prod, one)
                    nc.scalar.activation(cand[:, c, :], gate_bank[c][:], ACT.Tanh,
                                         bias=bias_v[:, c:c + 1]).then_inc(cand_made, 1)
                if name == "hT_hi":
                    act.wait_ge(h_new, one)
                    copy(hT_hi[:, c, :], hT[:, c, :], hT_hi_made)
                if name == "h_hi":
                    act.wait_ge(h_turned, nth(i, STEPS, s))
                    for n in range(C):
                        copy(h_hi[:, n, :], gate_bank[2 + n][:], h_hi_made)
                if name == "split_x":
                    split_x(i + 1)

            def attention(name, b, h, j):
                batch, head = nth(j, PAIR, b), nth(j, H, HEADS * b + h)
                if name == "x1T_hi":
                    act.wait_ge(x1_turned, batch)
                    copy(flat(x1T_hi), score_bank[0][:], x1T_hi_made)
                if name == "q":
                    act.wait_ge(q_prod, batch)
                    for c in range(C):
                        last = nc.scalar.activation(qT[:, c, :], score_bank[1][:, c * N:(c + 1) * N],
                                                    ACT.Identity, bias=bias_q[:, c:c + 1],
                                                    scale=-SCORE_SCALE)
                    last.then_inc(q_made, 1)
                    act.wait_ge(q_made, batch)
                    copy(flat(qT_s[0]), flat(qT), q_hi_made)
                if name == "k":
                    act.wait_ge(k_prod, batch)
                    for c in range(C):
                        last = nc.scalar.activation(kT[:, c, :], turn_bank[:, c * N:(c + 1) * N],
                                                    ACT.Identity, bias=raw_bias[:, 6, c:c + 1])
                    last.then_inc(k_made, 1)
                    act.wait_ge(k_made, batch)
                    copy(flat(kT_s[0]), flat(kT), k_hi_made)
                if name == "v_hi":
                    act.wait_ge(v_made, batch)
                    act.wait_ge(pads_zero, 2)
                    copy(windows(v_s[0]), by_head(v_sb), v_hi_made)
                if name == "exp":
                    act.wait_ge(masked, from_one(head))
                    for n in range(C):
                        last = nc.scalar.activation(
                            probs[:, h % 2, n, :], neg_scores[:, h % 2, n, :], ACT.Exp, scale=-1.0,
                            bias=neg_max[b][:, h, n:n + 1], accum_out=sums[b][:, h, n:n + 1])
                    last.then_inc(probs_made, 1)
                if name == "probsT_hi":
                    act.wait_ge(probs_turned, head)
                    act.wait_ge(mixed, from_one(lately(j, H, HEADS * b + h - 2)))
                    copy(probsT_s[0][:, h % 2].rearrange("p c n -> p (c n)"), turn_bank[:], probsT_hi_made)
                if name == "spread":
                    act.wait_ge(spread, batch)
                    copy(flat(spread_sb), turn_bank[:], spread_copied)
                if name == "oT_hi":
                    act.wait_ge(oT_made, batch)
                    copy(flat(oT_hi), flat(oT), oT_hi_made)

            GATED = ("u_copy", "a_hi", "r_tanh", "rh_hi", "z_tanh", "cand", "hT_hi", "h_hi", "split_x")

            def body(i, j):
                for name, a, b in plan:
                    if name in GATED:
                        if i is not None:
                            gated(name, a, b, i)
                    elif j is not None:
                        attention(name, a, b, j)

            iterations(act, body, prepare)

        @block.vector
        def _(dve):
            def rest(lo, full, hi, done):
                nc.vector.tensor_tensor(lo, full, hi.bitcast(f32), ALU.subtract).then_inc(done, 1)

            def split_x(i):
                for c in range(C):
                    dve.wait_ge(hT_hi_made, nth(i, G, c))
                    rest(hT_lo[:, c, :], xT_in[:, c, :], hT_hi[:, c, :], hT_lo_made)
                for c in range(C):
                    dve.wait_ge(h_hi_made, nth(i, G, c))
                    rest(h_lo[:, c, :], x_in[:, c, :], h_hi[:, c, :], h_lo_made)

            def prepare(which):
                for n in which:
                    _, name, chunks = all_weights[n]
                    st = stage[n % 3]
                    first = st[:, 0:C, :].rearrange("p c n -> p (c n)")
                    if name in CHANGED:
                        dve.wait_ge(stage_loaded[n % 3], 16 * (n // 3 + 1))
                        if chunks > C:
                            nc.vector.tensor_tensor(first, first, st[:, C:2 * C, :].rearrange("p c n -> p (c n)"),
                                                    ALU.add).then_inc(sum_ready, 1)
                        else:
                            nc.vector.tensor_scalar(first, first, 0.5, None, ALU.mult).then_inc(sum_ready, 1)
                    dve.wait_ge(hi_ready, n + 1)
                    nc.vector.tensor_tensor(flat(w_s[name][1]), first, flat(w_s[name][0]).bitcast(f32),
                                            ALU.subtract).then_inc(lo_ready, 1)

            for made in (masked, probsT_lo_made, y2_made):
                nc.vector.nop().then_inc(made, 1)
            nc.vector.memset(power[:], -0.5)
            split_x(0)
            prepare(SETUP)
            dve.wait_ge(small_loaded, 16 * SMALL)
            nc.vector.tensor_tensor(bias_r[:], raw_bias[:, 1, :], raw_bias[:, 3, :], ALU.add)
            nc.vector.tensor_tensor(bias_z[:], raw_bias[:, 0, :], raw_bias[:, 3, :], ALU.add)
            nc.vector.tensor_tensor(bias_v[:], raw_bias[:, 2, :], raw_bias[:, 4, :], ALU.add)
            nc.vector.tensor_scalar(flat(mask), flat(mask), -1.0, 1.0, ALU.mult, ALU.add).then_inc(bias_step, 1)
            dve.wait_ge(bias_step, 1)
            nc.vector.tensor_scalar(flat(mask), flat(mask), MASK, None, ALU.mult)
            nc.vector.tensor_scalar(bias_r[:], bias_r[:], 0.5, None, ALU.mult)
            nc.vector.tensor_scalar(bias_z[:], bias_z[:], 0.5, None, ALU.mult)
            nc.vector.tensor_scalar(bias_q[:], raw_bias[:, 5, :], -SCORE_SCALE, None,
                                    ALU.mult).then_inc(bias_ready, 1)

            plan = plan_after(VECTOR_ORDER)

            def gated(name, s, c, i):
                one = nth(i, G, C * s + c)

                def h_old():
                    return hT[:, c, :] if s else xT_in[:, c, :]

                if name == "a_lo":
                    dve.wait_ge(a_hi_made, one)
                    rest(aT_lo[:, c, :], gate_bank[2 + c][:], aT_hi[:, c, :], a_lo_made)
                if name == "r_sum":
                    dve.wait_ge(r_prod, one)
                    dve.wait_ge(u_copied, one)
                    nc.vector.tensor_tensor(r_tanh[:, c, :], gate_bank[c][:], uT[:, c, :],
                                            ALU.add).then_inc(r_summed, 1)
                if name == "rh":
                    dve.wait_ge(r_tanh_made, one)
                    wait_ge(dve, rh_lo_made, lately(i, G, C * (s - 1) + c))
                    nc.vector.scalar_tensor_tensor(out=rhT[:, c, :], in0=r_tanh[:, c, :], scalar=1.0,
                                                   in1=h_old(), op0=ALU.add,
                                                   op1=ALU.mult).then_inc(rh_made, 1)
                if name == "z_sum":
                    dve.wait_ge(z_prod, one)
                    nc.vector.tensor_tensor(z_tanh[:, c, :], gate_bank[2 + c][:], uT[:, c, :],
                                            ALU.add).then_inc(z_summed, 1)
                if name == "gate":
                    dve.wait_ge(z_tanh_made, one)
                    nc.vector.tensor_scalar(gate[:, c, :], z_tanh[:, c, :], 0.5, 0.5, ALU.mult,
                                            ALU.add).then_inc(gate_made, 1)
                if name == "move":
                    dve.wait_ge(gate_made, one)
                    dve.wait_ge(cand_made, one)
                    nc.vector.tensor_tensor(cand[:, c, :], gate[:, c, :], cand[:, c, :],
                                            ALU.mult).then_inc(move_made, 1)
                if name == "h_new":
                    dve.wait_ge(kept_made, one)
                    dve.wait_ge(move_made, one)
                    nc.vector.tensor_tensor(hT[:, c, :], kept[:, c, :], cand[:, c, :],
                                            ALU.add).then_inc(h_new, 1)
                if name == "hT_lo":
                    dve.wait_ge(hT_hi_made, nth(i, G, C * (s + 1) + c))
                    rest(hT_lo[:, c, :], hT[:, c, :], hT_hi[:, c, :], hT_lo_made)
                if name == "h_lo":
                    for n in range(C):
                        dve.wait_ge(h_hi_made, nth(i, G, C * (s + 1) + n))
                        rest(h_lo[:, n, :], gate_bank[2 + n][:], h_hi[:, n, :], h_lo_made)
                if name == "split_x":
                    split_x(i + 1)
                if name == "y1":
                    dve.wait_ge(h_turned, nth(i, STEPS, s))
                    dve.wait_ge(x_kept, nth(i, 1, 0))
                    for n in range(C):
                        nc.vector.tensor_tensor(y1[:, n].rearrange("p b n -> p (b n)"), gate_bank[2 + n][:],
                                                y1[:, n].rearrange("p b n -> p (b n)"),
                                                ALU.add).then_inc(y1_made, 1)
                    dve.wait_ge(y1_made, nth(i, C, C - 1))
                    for n in range(C):
                        for b in range(PAIR):
                            last = nc.vector.bn_stats(stats1[:, n * PAIR + b, :], y1[:, n, b, :])
                    last.then_inc(stats1_made, 1)
                    dve.wait_ge(stats1_made, nth(i, 1, 0))
                    stand_alone(dve)
                    for g in range(C * PAIR):
                        last = nc.vector.bn_aggr(mv1[:, g, :], stats1[:, g, :])
                    last.then_inc(mv1_made, 1)
                    dve.wait_ge(mv1_made, nth(i, 1, 0))
                    nc.vector.tensor_scalar(var1[:], mv1[:, :, 1], EPS, None, ALU.add).then_inc(var1_made, 1)
                if name == "norm1":
                    dve.wait_ge(rstd1_made, nth(i, 1, 0))
                    for n in range(C):
                        for b in range(PAIR):
                            g = n * PAIR + b
                            last = nc.vector.tensor_scalar(x1[:, n, b, :], y1[:, n, b, :], mv1[:, g, 0:1],
                                                           rstd1[:, g:g + 1], ALU.subtract, ALU.mult)
                    last.then_inc(x1_made, 1)

            def attention(name, b, h, j):
                batch, head = nth(j, PAIR, b), nth(j, H, HEADS * b + h)
                if name == "x1T_lo":
                    dve.wait_ge(x1T_hi_made, batch)
                    rest(flat(x1T_lo), score_bank[0][:], flat(x1T_hi), x1T_lo_made)
                if name == "q_lo":
                    dve.wait_ge(q_hi_made, batch)
                    rest(flat(qT_s[1]), flat(qT), flat(qT_s[0]), q_lo_made)
                if name == "k_lo":
                    dve.wait_ge(k_hi_made, batch)
                    rest(flat(kT_s[1]), flat(kT), flat(kT_s[0]), k_lo_made)
                if name == "v":
                    dve.wait_ge(v_out, batch)
                    nc.vector.tensor_tensor(v_sb[:], score_bank[0][:].rearrange("p (c n) -> p c n", c=C),
                                            bv_rows[:].unsqueeze(1).to_broadcast([P, C, D]),
                                            ALU.add).then_inc(v_made, 1)
                if name == "v_lo":
                    dve.wait_ge(v_hi_made, batch)
                    dve.wait_ge(pads_zero, 2)
                    rest(windows(v_s[1]), by_head(v_sb), windows(v_s[0]), v_lo_made)
                if name == "mask":
                    dve.wait_ge(scored, head)
                    dve.wait_ge(probs_made, from_one(lately(j, H, HEADS * b + h - 2)))
                    stand_alone(dve)
                    for n in range(C):
                        last = nc.vector.tensor_tensor_reduce(
                            out=neg_scores[:, h % 2, n, :], in0=score_bank[h % 2][:, n * N:(n + 1) * N],
                            in1=mask[:, n, :], scale=1.0, scalar=3.4e38, op0=ALU.add, op1=ALU.min,
                            accum_out=neg_max[b][:, h, n:n + 1])
                    last.then_inc(masked, 1)
                if name == "probsT_lo":
                    dve.wait_ge(probsT_hi_made, from_one(head))
                    rest(probsT_s[1][:, h % 2].rearrange("p c n -> p (c n)"), turn_bank[:],
                         probsT_s[0][:, h % 2].rearrange("p c n -> p (c n)"), probsT_lo_made)
                if name == "inverse":
                    dve.wait_ge(probs_made, from_one(head))
                    nc.vector.reciprocal(inverse[b][:], sums[b][:]).then_inc(inverse_made, 1)
                    dve.wait_ge(inverse_made, batch)
                    for n in range(C):
                        last = nc.vector.tensor_copy(
                            inverse_wide[:, n], inverse[b][:, :, n:n + 1].to_broadcast([P, HEADS, HEAD_DIM]))
                    last.then_inc(inverse_wide_made, 1)
                if name == "oT":
                    dve.wait_ge(spread_copied, from_one(batch))
                    dve.wait_ge(mixed, from_one(nth(j, H, HEADS * b + HEADS - 1)))
                    nc.vector.tensor_tensor(flat(oT), mix_bank[:], flat(spread_sb),
                                            ALU.mult).then_inc(oT_made, 1)
                if name == "oT_lo":
                    dve.wait_ge(oT_hi_made, batch)
                    rest(flat(oT_lo), flat(oT), flat(oT_hi), oT_lo_made)
                if name == "y2":
                    dve.wait_ge(o_prod, batch)
                    dve.wait_ge(x1_bo_made, batch)
                    dve.wait_ge(stored[b], from_one(j) * 16)
                    nc.vector.tensor_tensor(flat(y2[b]), mix_bank[:], flat(x1_bo[b]),
                                            ALU.add).then_inc(y2_made, 1)
                    dve.wait_ge(y2_made, from_one(batch))
                    for n in range(C):
                        last = nc.vector.bn_stats(stats2[b][:, n, :], y2[b][:, n, :])
                    last.then_inc(stats2_made, 1)
                    dve.wait_ge(stats2_made, batch)
                    stand_alone(dve)
                    for n in range(C):
                        last = nc.vector.bn_aggr(mv2[b][:, n, :], stats2[b][:, n, :])
                    last.then_inc(mv2_made, 1)
                    dve.wait_ge(mv2_made, batch)
                    nc.vector.tensor_scalar(var2[b][:], mv2[b][:, :, 1], EPS, None,
                                            ALU.add).then_inc(var2_made, 1)
                if name == "norm2":
                    dve.wait_ge(rstd2_made, batch)
                    for n in range(C):
                        last = nc.vector.tensor_scalar(y2[b][:, n, :], y2[b][:, n, :],
                                                       mv2[b][:, n, 0:1], rstd2[b][:, n:n + 1],
                                                       ALU.subtract, ALU.mult)
                    last.then_inc(out_made, 1)

            GATED = ("a_lo", "r_sum", "rh", "z_sum", "gate", "move", "h_new", "hT_lo", "h_lo", "split_x",
                     "y1", "norm1")

            def body(i, j):
                for name, a, b in plan:
                    if name in GATED:
                        if i is not None:
                            gated(name, a, b, i)
                    elif j is not None:
                        attention(name, a, b, j)

            iterations(dve, body, prepare)

        @block.gpsimd
        def _(pool):
            nc.gpsimd.memset(ident[:], 0.0).then_inc(ident_zero, 1)
            pool.wait_ge(ident_zero, 1)
            nc.gpsimd.affine_select(out=ident[:], in_=ident[:], compare_op=ALU.not_equal, fill=1.0, base=0,
                                    pattern=[[-1, P]], channel_multiplier=1).then_inc(ident_ready, 1)
            for part in v_s:
                nc.gpsimd.memset(part[:].bitcast(f32), 0.0).then_inc(pads_zero, 1)
            pool.wait_ge(small_loaded, 16 * SMALL)

            plan = plan_after(POOL_ORDER)

            def gated(name, s, c, i):
                one = nth(i, G, C * s + c)
                if name == "keep_x":
                    pool.wait_ge(x_loaded, nth(i, 2 * PAIR, 2 * PAIR - 1) * 16)
                    wait_ge(pool, x1_made, nth(i, 1, -1))
                    stand_alone(pool)
                    nc.gpsimd.tensor_copy(y1[:].rearrange("p c b n -> p c (b n)"), x_in[:]).then_inc(x_kept, 1)
                if name == "rh_lo":
                    pool.wait_ge(rh_hi_made, one)
                    nc.gpsimd.tensor_tensor(rhT_lo[:, c, :], rhT[:, c, :], rhT_hi[:, c, :].bitcast(f32),
                                            ALU.subtract).then_inc(rh_lo_made, 1)
                if name == "keep":
                    pool.wait_ge(z_tanh_made, one)
                    wait_ge(pool, h_new, lately(i, G, C * (s - 1) + c))
                    stand_alone(pool)
                    nc.gpsimd.tensor_scalar(kept[:, c, :], z_tanh[:, c, :], -0.5, 0.5, ALU.mult,
                                            ALU.add).then_inc(keep_made, 1)
                    pool.wait_ge(keep_made, one)
                    nc.gpsimd.tensor_tensor(kept[:, c, :], kept[:, c, :],
                                            hT[:, c, :] if s else xT_in[:, c, :],
                                            ALU.mult).then_inc(kept_made, 1)
                if name == "norm1":
                    pool.wait_ge(var1_made, nth(i, 1, 0))
                    nc.gpsimd.tensor_tensor(rstd1[:], var1[:], power[:], ALU.pow).then_inc(rstd1_made, 1)

            def attention(name, b, j):
                batch = nth(j, PAIR, b)
                if name == "x1_bo":
                    pool.wait_ge(x1_made, nth(j, 1, 0))
                    pool.wait_ge(y2_made, from_one(nth(j, PAIR, -1)))
                    nc.gpsimd.tensor_tensor(x1_bo[b][:], x1[:, :, b, :],
                                            bo_rows[:].unsqueeze(1).to_broadcast([P, C, D]),
                                            ALU.add).then_inc(x1_bo_made, 1)
                if name == "norm2":
                    pool.wait_ge(var2_made, batch)
                    nc.gpsimd.tensor_tensor(rstd2[b][:], var2[b][:], power[:, 0:C],
                                            ALU.pow).then_inc(rstd2_made, 1)

            def body(i, j):
                for name, a, b in plan:
                    if name in ("keep_x", "rh_lo", "keep", "norm1"):
                        if i is not None:
                            gated(name, a, b, i)
                    elif j is not None:
                        attention(name, a, j)

            iterations(pool, body)


def kernel(**inputs):
    import numpy as np
    import concourse.bacc as bacc
    from concourse import mybir as mb
    from concourse.bass_utils import run_bass_kernel_spmd

    def turned(a):
        return np.ascontiguousarray(np.swapaxes(a, -1, -2))

    g0, g1 = "L0_gnn_", "L1_gnn_"
    arrays = {"x": inputs["x"], "xT": turned(inputs["x"]), "adj": inputs["adj"], "adjT": turned(inputs["adj"])}
    for n in ("w3", "u3", "w4", "w5", "u5"):
        arrays[n + "T"] = turned(inputs[f"{g0}{n}_w"])
        arrays[n + "b"] = inputs[f"{g0}{n}_b"]
    for n in "qkvo":
        arrays["w" + n] = inputs[f"{g1}W{n}"]
        arrays["b" + n] = inputs[f"{g1}b{n}"]
    for n in ("w3b", "w4b", "w5b", "u3b", "u5b", "bq", "bk"):
        arrays[n] = turned(arrays[n].reshape(C, P))
    arrays = {n: np.ascontiguousarray(a) for n, a in arrays.items()}

    nc = bacc.Bacc("TRN2", target_bir_lowering=False, num_devices=1)
    args = {n: nc.dram_tensor(n, a.shape, mb.dt.from_np(a.dtype), kind="ExternalInput").ap()
            for n, a in arrays.items()}
    out = nc.dram_tensor("out", arrays["x"].shape, mb.dt.float32, kind="ExternalOutput").ap()
    build(nc, out=out, **args)
    return run_bass_kernel_spmd(nc, [arrays], core_ids=[0]).results[0]["out"]
```

```python
from contextlib import ExitStack

import concourse.bass as bass
from concourse import mybir

P = 128
BATCHES, N, D, STEPS = 32, 256, 256, 3
HEADS = 8
HEAD_DIM = D // HEADS
PAIR = 2
PAIRS = BATCHES // PAIR
C = D // P
HEADS_PER_CHUNK = P // HEAD_DIM
EPS = 1e-5
SMALL = 10
MASK = 1e9
SCORE_SCALE = float(HEAD_DIM) ** -0.5


def in_order(text):
    return [(name, int(at[0]), int(at[1])) for name, at in (piece.split(":") for piece in text.split())]


TENSOR_ORDER = in_order("""
    u:00 u:01 a:00 x1:00 a:01 q:00 r:00 r:01 z:00 z:01 k:00 v:00 v:01 w:00 w:01 t:00 vv:00 t:01 u:10
    u:11 score:00 score:01 a:10 turn:00 score:02 a:11 turn:01 score:03 mix:00 turn:02 mix:01 score:04
    turn:03 score:05 mix:02 turn:04 score:06 mix:03 turn:05 score:07 r:10 mix:04 turn:06 mix:05 x1:10
    turn:07 mix:06 q:10 r:11 z:10 mix:07 k:10 z:11 spread:00 v:10 v:11 w:10 w:11 vv:10 t:10 o:00 t:11
    u:20 u:21 a:20 score:10 score:11 a:21 turn:10 score:12 turn:11 score:13 mix:10 r:20 turn:12 r:21
    mix:11 score:14 turn:13 mix:12 score:15 z:20 turn:14 mix:13 z:21 score:16 turn:15 score:17 v:20
    mix:14 turn:16 v:21 w:20 mix:15 turn:17 w:21 mix:16 mix:17 spread:10 t:20 t:21 o:10
""")
SCALAR_ORDER = in_order("""
    u_copy:00 x1T_hi:00 a_hi:00 u_copy:01 a_hi:01 q:00 r_tanh:00 r_tanh:01 rh_hi:00 z_tanh:00 rh_hi:01
    z_tanh:01 k:00 cand:00 cand:01 hT_hi:00 hT_hi:01 h_hi:01 v_hi:00 exp:00 a_hi:10 probsT_hi:00 exp:01
    u_copy:10 probsT_hi:01 exp:02 a_hi:11 probsT_hi:02 exp:03 u_copy:11 probsT_hi:03 exp:04 probsT_hi:04
    exp:05 probsT_hi:05 exp:06 exp:07 probsT_hi:06 x1T_hi:10 r_tanh:10 rh_hi:10 probsT_hi:07 q:10
    z_tanh:10 r_tanh:11 k:10 rh_hi:11 spread:00 z_tanh:11 oT_hi:00 cand:10 cand:11 hT_hi:10 hT_hi:11
    h_hi:11 u_copy:20 v_hi:10 u_copy:21 a_hi:20 exp:10 a_hi:21 probsT_hi:10 exp:11 exp:12 probsT_hi:11
    split_x:21 probsT_hi:12 exp:13 probsT_hi:13 exp:14 r_tanh:20 r_tanh:21 probsT_hi:14 exp:15 rh_hi:20
    rh_hi:21 probsT_hi:15 exp:16 z_tanh:20 z_tanh:21 probsT_hi:16 exp:17 probsT_hi:17 cand:20 cand:21
    spread:10 oT_hi:10
""")
VECTOR_ORDER = in_order("""
    x1T_lo:00 a_lo:00 a_lo:01 r_sum:00 r_sum:01 q_lo:00 rh:00 rh:01 z_sum:00 z_sum:01 gate:00 k_lo:00
    move:00 gate:01 h_new:00 move:01 h_new:01 hT_lo:00 hT_lo:01 h_lo:01 v:00 mask:00 mask:01 v_lo:00
    probsT_lo:00 mask:02 probsT_lo:01 mask:03 a_lo:10 probsT_lo:02 mask:04 a_lo:11 probsT_lo:03 mask:05
    probsT_lo:04 mask:06 mask:07 probsT_lo:05 r_sum:10 probsT_lo:06 x1T_lo:10 rh:10 probsT_lo:07
    inverse:07 r_sum:11 q_lo:10 z_sum:10 rh:11 z_sum:11 oT:00 k_lo:10 oT_lo:00 gate:10 gate:11 move:10
    h_new:10 move:11 h_new:11 hT_lo:10 hT_lo:11 h_lo:11 v:10 y2:00 mask:10 mask:11 a_lo:20 v_lo:10
    probsT_lo:10 mask:12 a_lo:21 probsT_lo:11 mask:13 probsT_lo:12 r_sum:20 mask:14 r_sum:21
    probsT_lo:13 mask:15 rh:20 rh:21 probsT_lo:14 z_sum:20 z_sum:21 mask:16 probsT_lo:15 mask:17
    split_x:21 probsT_lo:16 inverse:17 gate:20 probsT_lo:17 move:20 gate:21 move:21 h_new:20 oT:10
    h_new:21 oT_lo:10 y1:21 y2:10 norm1:21 norm2:00 norm2:10
""")
POOL_ORDER = in_order("""
    keep_x:00 rh_lo:00 rh_lo:01 keep:00 keep:01 x1_bo:00 rh_lo:10 keep:10 rh_lo:11 keep:11 rh_lo:20
    rh_lo:21 keep:20 norm2:00 x1_bo:10 keep:21 norm1:21 norm2:10
""")
DMA_ORDER = in_order("""
    q_stack:00 k_stack:00 load:01 q_stack:10 k_stack:10 store:00 store:10
""")
Q_PARTS, K_PARTS = ("hi", "hi", "lo"), ("hi", "lo", "hi")
STACK = len(Q_PARTS) * HEAD_DIM
WINDOW = P - HEAD_DIM


def nth(i, per_iteration, k):
    return i * per_iteration + (k + 1)


def lately(i, per_iteration, k):
    return nth(i, per_iteration, max(k, -1))


def from_one(count):
    return count + 1


def build(nc, x, xT, adj, adjT, w3T, w3b, u3T, u3b, w4T, w4b, w5T, w5b, u5T, u5b,
          wq, bq, wk, bk, wv, bv, wo, bo, out):
    f32, f32r = mybir.dt.float32, mybir.dt.float32r
    ALU, ACT = mybir.AluOpType, mybir.ActivationFunctionType
    G = STEPS * C
    H = PAIR * HEADS
    HC = H * C

    ctx = ExitStack()
    with ctx:
        def sb(name, shape, dt=f32):
            return ctx.enter_context(nc.sbuf_tensor(name, shape, dt))

        def parts(name, shape):
            return sb(name + "_hi", shape, f32r), sb(name + "_lo", shape, f32r)

        def sem(name):
            return ctx.enter_context(nc.semaphore(name))

        def bank(name):
            return ctx.enter_context(nc.psum_tensor(name, [P, 512], f32))

        stage = [sb(f"stage{n}", [P, 2 * C, D]) for n in range(3)]
        w_s = {n: parts(n, [P, C, D])
               for n in ("adjT", "w3", "w4", "w5", "u3", "u5", "wq", "wk", "wv", "wo")}
        mask = sb("mask", [P, C, N])
        ident = sb("ident", [P, P])
        power = sb("power", [P, C * PAIR])
        raw_bias = sb("raw_bias", [P, 7, C])
        bias_r, bias_z, bias_v = sb("bias_r", [P, C]), sb("bias_z", [P, C]), sb("bias_v", [P, C])
        bias_q = sb("bias_q", [P, C])
        bv_rows, bo_rows = sb("bv_rows", [P, D]), sb("bo_rows", [P, D])
        wide = [P, C, PAIR * N]
        x_in, xT_in = sb("x_in", wide), sb("xT_in", wide)
        h_hi, h_lo = parts("h", wide)
        hT = sb("hT", wide)
        hT_hi, hT_lo = parts("hT", wide)
        aT_hi, aT_lo = parts("aT", wide)
        uT = sb("uT", wide)
        r_tanh, z_tanh = sb("r_tanh", wide), sb("z_tanh", wide)
        rhT = sb("rhT", wide)
        rhT_hi, rhT_lo = parts("rhT", wide)
        gate, kept = r_tanh, sb("kept", wide)
        cand = sb("cand", wide)
        y1 = sb("y1", [P, C, PAIR, D])
        x1 = sb("x1", [P, C, PAIR, D])
        stats1, mv1 = sb("stats1", [P, C * PAIR, 6]), sb("mv1", [P, C * PAIR, 2])
        var1, rstd1 = sb("var1", [P, C * PAIR]), sb("rstd1", [P, C * PAIR])
        x1_bo = [sb(f"x1_bo{b}", [P, C, D]) for b in range(PAIR)]
        y2 = [sb(f"y2_{b}", [P, C, D]) for b in range(PAIR)]
        stats2 = [sb(f"stats2_{b}", [P, C, 6]) for b in range(PAIR)]
        mv2 = [sb(f"mv2_{b}", [P, C, 2]) for b in range(PAIR)]
        var2 = [sb(f"var2_{b}", [P, C]) for b in range(PAIR)]
        rstd2 = [sb(f"rstd2_{b}", [P, C]) for b in range(PAIR)]
        x1T_hi, x1T_lo = parts("x1T", [P, C, N])
        qT, kT = sb("qT", [P, C, N]), sb("kT", [P, C, N])
        qT_s, kT_s = parts("qT", [P, C, N]), parts("kT", [P, C, N])
        q_stack, k_stack = sb("q_stack", [STACK, C, HEADS_PER_CHUNK, N], f32r), sb(
            "k_stack", [STACK, C, HEADS_PER_CHUNK, N], f32r)
        v_sb = sb("v_sb", [P, C, D])
        v_s = parts("v", [P, C, C, HEADS_PER_CHUNK, P])
        neg_scores, probs = (stage[n][:].rearrange("p (a c) n -> p a c n", c=C) for n in range(2))
        spread_sb, oT = stage[2][:, 0:C, :], stage[2][:, C:2 * C, :]
        neg_max = [sb(f"neg_max{b}", [P, HEADS, C]) for b in range(PAIR)]
        sums = [sb(f"sums{b}", [P, HEADS, C]) for b in range(PAIR)]
        inverse = [sb(f"inverse{b}", [P, HEADS, C]) for b in range(PAIR)]
        inverse_wide = sb("inverse_wide", [P, C, HEADS, HEAD_DIM])
        probsT_s = parts("probsT", [P, 2, C, N])
        oT_hi, oT_lo = parts("oT", [P, C, N])

        gate_bank = [bank(f"gate_bank{n}") for n in range(4)]
        score_bank = [bank(f"score_bank{n}") for n in range(2)]
        turn_bank, mix_bank = bank("turn_bank"), bank("mix_bank")

        stage_loaded = [sem(f"stage_loaded{n}") for n in range(3)]
        small_loaded = sem("small_loaded")
        hi_ready, lo_ready, sum_ready = sem("hi_ready"), sem("lo_ready"), sem("sum_ready")
        ident_zero, ident_ready, pads_zero = sem("ident_zero"), sem("ident_ready"), sem("pads_zero")
        bias_step, bias_ready = sem("bias_step"), sem("bias_ready")
        x_loaded, x_kept = sem("x_loaded"), sem("x_kept")
        stored = [sem(f"stored{b}") for b in range(PAIR)]
        u_prod, a_prod, r_prod, z_prod, v_prod, h_turned = (
            sem("u_prod"), sem("a_prod"), sem("r_prod"), sem("z_prod"), sem("v_prod"), sem("h_turned"))
        u_copied, a_hi_made, a_lo_made = sem("u_copied"), sem("a_hi_made"), sem("a_lo_made")
        r_summed, r_tanh_made, rh_made = sem("r_summed"), sem("r_tanh_made"), sem("rh_made")
        rh_hi_made, rh_lo_made = sem("rh_hi_made"), sem("rh_lo_made")
        z_summed, z_tanh_made, gate_made = sem("z_summed"), sem("z_tanh_made"), sem("gate_made")
        keep_made, kept_made = sem("keep_made"), sem("kept_made")
        cand_made, move_made, h_new = sem("cand_made"), sem("move_made"), sem("h_new")
        hT_hi_made, hT_lo_made, h_hi_made, h_lo_made = (
            sem("hT_hi_made"), sem("hT_lo_made"), sem("h_hi_made"), sem("h_lo_made"))
        y1_made, stats1_made, mv1_made, var1_made, rstd1_made, x1_made = (
            sem("y1_made"), sem("stats1_made"), sem("mv1_made"), sem("var1_made"), sem("rstd1_made"),
            sem("x1_made"))
        x1_turned, q_prod, k_prod, v_out = sem("x1_turned"), sem("q_prod"), sem("k_prod"), sem("v_out")
        scored, probs_turned, mixed, spread, o_prod = (
            sem("scored"), sem("probs_turned"), sem("mixed"), sem("spread"), sem("o_prod"))
        x1T_hi_made, x1T_lo_made = sem("x1T_hi_made"), sem("x1T_lo_made")
        q_made, k_made, v_made = sem("q_made"), sem("k_made"), sem("v_made")
        q_hi_made, k_hi_made, q_lo_made, k_lo_made = (
            sem("q_hi_made"), sem("k_hi_made"), sem("q_lo_made"), sem("k_lo_made"))
        v_hi_made, v_lo_made = sem("v_hi_made"), sem("v_lo_made")
        q_stacked, k_stacked = sem("q_stacked"), sem("k_stacked")
        masked, probs_made = sem("masked"), sem("probs_made")
        probsT_hi_made, probsT_lo_made = sem("probsT_hi_made"), sem("probsT_lo_made")
        inverse_made, inverse_wide_made, spread_copied = (
            sem("inverse_made"), sem("inverse_wide_made"), sem("spread_copied"))
        oT_made, oT_hi_made, oT_lo_made = sem("oT_made"), sem("oT_hi_made"), sem("oT_lo_made")
        x1_bo_made, y2_made, stats2_made, mv2_made, var2_made, rstd2_made, out_made = (
            sem("x1_bo_made"), sem("y2_made"), sem("stats2_made"), sem("mv2_made"), sem("var2_made"),
            sem("rstd2_made"), sem("out_made"))

        def flat(t):
            return t[:, :, :].rearrange("p c n -> p (c n)")

        def wait_ge(engine, semaphore, value):
            if not isinstance(value, int) or value > 0:
                engine.wait_ge(semaphore, value)

        def stand_alone(engine):
            engine.nop(nofuse=True)

        def windows(v_part):
            return v_part[:].rearrange("p a c r w -> p (a c) r w")[:, :, :, WINDOW:P]

        def by_head(t):
            return t[:].rearrange("p a (c r d) -> p (a c) r d", r=HEADS_PER_CHUNK, d=HEAD_DIM)

        gated_weights = [(u3T, "u3", C), (adjT, "adjT", C), (w4T, "w4", 2 * C), (w3T, "w3", 2 * C),
                         (w5T, "w5", 2 * C), (u5T, "u5", C)]
        all_weights = gated_weights + [(wq, "wq", C), (wk, "wk", C), (wv, "wv", C), (wo, "wo", C)]
        order_of = {name: n for n, (_, name, _) in enumerate(all_weights)}
        CHANGED = ("w4", "w3", "w5", "u5")
        SETUP = range(len(gated_weights))
        AT_STEP = {1: range(len(gated_weights), len(all_weights) - 1),
                   2: range(len(all_weights) - 1, len(all_weights))}

        def iterations(engine, body):
            body(0, None)
            with engine.Fori(0, PAIRS - 1) as j:
                body(j + 1, j)
            body(None, PAIRS - 1)

        block = ctx.enter_context(nc.Block())

        @block.sync
        def _(sp):
            def load_pair(i):
                for b in range(PAIR):
                    at = bass.ds(i * PAIR + b, 1)
                    sp.dma_start(xT_in[:, :, b * N:(b + 1) * N],
                                 xT[at].rearrange("b (c p) n -> p (b c) n", p=P)).then_inc(x_loaded, 16)
                    sp.dma_start(x_in[:, :, b * D:(b + 1) * D],
                                 x[at].rearrange("b (c p) d -> p (b c) d", p=P)).then_inc(x_loaded, 16)

            def free_input(i):
                sp.wait_ge(h_lo_made, nth(i, G, C - 1))
                sp.wait_ge(hT_lo_made, nth(i, G, C - 1))
                sp.wait_ge(h_new, nth(i, G, C - 1))
                stand_alone(sp)
                sp.wait_ge(x_kept, nth(i, 1, 0))
                stand_alone(sp)

            for made in stored:
                sp.nop().then_inc(made, 16)
            load_pair(0)
            for n, (src, _, chunks) in enumerate(all_weights):
                if n >= 3:
                    sp.wait_ge(lo_ready, n - 2)
                sp.dma_start(stage[n % 3][:, 0:chunks, :],
                             src.rearrange("(c p) n -> p c n", p=P)).then_inc(stage_loaded[n % 3], 16)
                if n == 2:
                    for m, bias in enumerate((w3b, w4b, w5b, u3b, u5b, bq, bk)):
                        sp.dma_start(raw_bias[:, m, :], bias).then_inc(small_loaded, 16)
                    sp.dma_start(bv_rows[:], bv.partition_broadcast(P)).then_inc(small_loaded, 16)
                    sp.dma_start(bo_rows[:], bo.partition_broadcast(P)).then_inc(small_loaded, 16)
                    sp.dma_start(mask[:], adj.rearrange("(c p) n -> p c n", p=P)).then_inc(small_loaded, 16)

            free_input(0)
            load_pair(1)

            plan = DMA_ORDER

            def stack(dst, source, order, part, stacked):
                for p in [p for p, of in enumerate(order) if of == part]:
                    for r in range(HEADS_PER_CHUNK):
                        rows = slice(r * HEAD_DIM, (r + 1) * HEAD_DIM)
                        sp.dma_start(dst[p * HEAD_DIM:(p + 1) * HEAD_DIM, :, r, :].bitcast(f32),
                                     source[part == "lo"][rows, :, :].bitcast(f32)).then_inc(stacked, 16)

            def body(i, j, after=None):
                for name, b, _ in plan:
                    if name == "load" and i is not None:
                        free_input(i)
                        load_pair(after)
                    if j is None:
                        continue
                    if i is None and name != "store":
                        continue
                    if name == "q_stack":
                        sp.wait_ge(q_hi_made, nth(j, PAIR, b))
                        stack(q_stack, qT_s, Q_PARTS, "hi", q_stacked)
                        sp.wait_ge(q_lo_made, nth(j, PAIR, b))
                        stack(q_stack, qT_s, Q_PARTS, "lo", q_stacked)
                    if name == "k_stack":
                        sp.wait_ge(k_hi_made, nth(j, PAIR, b))
                        stack(k_stack, kT_s, K_PARTS, "hi", k_stacked)
                        sp.wait_ge(k_lo_made, nth(j, PAIR, b))
                        stack(k_stack, kT_s, K_PARTS, "lo", k_stacked)
                    if name == "store":
                        sp.wait_ge(out_made, nth(j, PAIR, b))
                        stand_alone(sp)
                        sp.dma_start(out[bass.ds(j * PAIR + b, 1)].rearrange("b (c p) d -> p (b c) d", p=P),
                                     y2[b][:]).then_inc(stored[b], 16)

            with sp.Fori(0, PAIRS - 2) as j:
                body(j + 1, j, j + 2)
            body(PAIRS - 1, PAIRS - 2, 0)
            body(None, PAIRS - 1)
            for b in range(PAIR):
                sp.wait_ge(stored[b], from_one(PAIRS) * 16)

        @block.tensor
        def _(pe):
            TERMS = ((0, 0), (0, 1), (1, 0))

            def product(psum, left, right, left_at, right_at, start=True, stop=True, late=1, low=None):
                passes = sorted(((l, r, c) for c in range(C) for l, r in TERMS), key=lambda of: of[late])
                for n, (l, r, c) in enumerate(passes):
                    if low and n == len(passes) - C:
                        pe.wait_ge(*low)
                    last = nc.tensor.matmul(psum, left_at(left[l], c), right_at(right[r], c),
                                            start=(start and n == 0),
                                            stop=(stop and n == len(passes) - 1), skip_group_check=True)
                return last

            def columns(k):
                return lambda t, c: t[:, c, k * P:(k + 1) * P]

            def whole(t, c):
                return t[:, c, :]

            def weight(name, i, s, c):
                if isinstance(i, int) and s == 0 and c == 0:
                    pe.wait_ge(lo_ready, order_of[name] + 1)
                return w_s[name]

            def gated(name, s, c, i):
                both, one = nth(i, G, C * s + 1), nth(i, G, C * s + c)
                if name == "u":
                    pe.wait_ge(hT_hi_made, both)
                    wait_ge(pe, cand_made, lately(i, G, C * (s - 1) + c))
                    product(gate_bank[c][:], weight("u3", i, s, c), (hT_hi, hT_lo), columns(c),
                            whole, low=(hT_lo_made, both)).then_inc(u_prod, 1)
                if name == "a":
                    pe.wait_ge(h_hi_made, both)
                    pe.wait_ge(h_lo_made, both)
                    if s == 0:
                        wait_ge(pe, y1_made, nth(i, C, -1))
                    adj_s = weight("adjT", i, s, c)
                    for b in range(PAIR):
                        last = product(gate_bank[2 + c][:, b * N:(b + 1) * N], (h_hi, h_lo), adj_s,
                                       columns(b * C + c), whole)
                    last.then_inc(a_prod, 1)
                if name == "r":
                    pe.wait_ge(a_hi_made, both)
                    pe.wait_ge(u_copied, one)
                    product(gate_bank[c][:], weight("w4", i, s, c), (aT_hi, aT_lo), columns(c),
                            whole, low=(a_lo_made, both)).then_inc(r_prod, 1)
                if name == "z":
                    product(gate_bank[2 + c][:], weight("w3", i, s, c), (aT_hi, aT_lo), columns(c),
                            whole).then_inc(z_prod, 1)
                if name == "v":
                    pe.wait_ge(r_summed, one)
                    product(gate_bank[c][:], weight("w5", i, s, c), (aT_hi, aT_lo), columns(c), whole,
                            stop=False)
                if name == "w":
                    pe.wait_ge(rh_hi_made, both)
                    product(gate_bank[c][:], weight("u5", i, s, c), (rhT_hi, rhT_lo), columns(c), whole,
                            start=False, low=(rh_lo_made, both)).then_inc(v_prod, 1)
                if name == "t":
                    if c == 0:
                        pe.wait_ge(z_summed, both)
                    pe.wait_ge(h_new, one)
                    for n in range(C):
                        for b in range(PAIR):
                            last = nc.tensor.matmul(
                                gate_bank[2 + n][:, b * D + c * P:b * D + (c + 1) * P],
                                hT[:, c, b * N + n * P:b * N + (n + 1) * P], ident[:],
                                is_transpose=True, start=True, stop=True)
                    if c == C - 1:
                        last.then_inc(h_turned, 1)

            def attention(name, b, h, j, stacked):
                batch, head = nth(j, PAIR, b), nth(j, H, HEADS * b + h)
                c, r = divmod(h, HEADS_PER_CHUNK)
                before = from_one(nth(j, H, HEADS * b - 1))
                if name == "x1":
                    pe.wait_ge(lo_ready, len(all_weights))
                    pe.wait_ge(x1_made, nth(j, 1, 0))
                    pe.wait_ge(masked, from_one(nth(j, HC, HEADS * b * C - 1)))
                    for c in range(C):
                        for n in range(C):
                            last = nc.tensor.matmul(
                                score_bank[0][:, c * N + n * P:c * N + (n + 1) * P],
                                x1[:, n, b, c * P:(c + 1) * P], ident[:],
                                is_transpose=True, start=True, stop=True)
                    last.then_inc(x1_turned, 1)
                if name == "q":
                    pe.wait_ge(x1T_hi_made, batch)
                    for c in range(C):
                        last = product(score_bank[1][:, c * N:(c + 1) * N], w_s["wq"],
                                       (x1T_hi, x1T_lo), columns(c), whole, low=(x1T_lo_made, batch))
                    last.then_inc(q_prod, 1)
                if name == "k":
                    pe.wait_ge(probsT_hi_made, before)
                    pe.wait_ge(probsT_lo_made, before)
                    for c in range(C):
                        last = product(turn_bank[:, c * N:(c + 1) * N], w_s["wk"],
                                       (x1T_hi, x1T_lo), columns(c), whole)
                    last.then_inc(k_prod, 1)
                if name == "vv":
                    for n in range(C):
                        last = product(score_bank[0][:, n * D:(n + 1) * D], (x1T_hi, x1T_lo),
                                       w_s["wv"], columns(n), whole)
                    last.then_inc(v_out, 1)
                if name == "score":
                    if h == 0:
                        if stacked:
                            pe.wait_ge(q_stacked, batch * 16 * len(Q_PARTS) * HEADS_PER_CHUNK)
                            pe.wait_ge(k_stacked, batch * 16 * len(K_PARTS) * HEADS_PER_CHUNK)
                        else:
                            for made in (q_hi_made, q_lo_made, k_hi_made, k_lo_made):
                                pe.wait_ge(made, batch)
                        pe.wait_ge(v_made, batch)
                    if h >= 2:
                        pe.wait_ge(masked, from_one(nth(j, HC, (HEADS * b + h - 1) * C - 1)))
                    rows = slice(r * HEAD_DIM, (r + 1) * HEAD_DIM)
                    for n in range(C):
                        scores = score_bank[h % 2][:, n * N:(n + 1) * N]
                        if stacked:
                            last = nc.tensor.matmul(scores, q_stack[:, c, r, n * P:(n + 1) * P],
                                                    k_stack[:, c, r, :], start=True, stop=True)
                            continue
                        for m, (left, right) in enumerate(TERMS):
                            last = nc.tensor.matmul(
                                scores, qT_s[left][rows, c, n * P:(n + 1) * P], kT_s[right][rows, c, :],
                                start=(m == 0), stop=(m == len(TERMS) - 1))
                    last.then_inc(scored, 1)
                if name == "turn":
                    if h == 0:
                        pe.wait_ge(k_made, batch)
                        pe.wait_ge(spread_copied, from_one(nth(j, PAIR, b - 1)))
                    else:
                        pe.wait_ge(probsT_hi_made, from_one(nth(j, H, HEADS * b + h - 1)))
                        pe.wait_ge(probsT_lo_made, from_one(nth(j, H, HEADS * b + h - 1)))
                    for n in range(C):
                        pe.wait_ge(probs_made, from_one(nth(j, HC, (HEADS * b + h) * C + n)))
                        for m in range(C):
                            last = nc.tensor.matmul(
                                turn_bank[:, m * N + n * P:m * N + (n + 1) * P],
                                probs[:, h % 2, n, m * P:(m + 1) * P], ident[:],
                                is_transpose=True, start=True, stop=True)
                    last.then_inc(probs_turned, 1)
                if name == "mix":
                    pe.wait_ge(probsT_hi_made, from_one(head))
                    if h == 0:
                        pe.wait_ge(v_lo_made, batch)
                        pe.wait_ge(y2_made, from_one(nth(j, PAIR, b - 1)))
                    window = slice(r * WINDOW + WINDOW, r * WINDOW + WINDOW + P)
                    last = product(mix_bank[:, c * N:(c + 1) * N], v_s, probsT_s,
                                   lambda t, a: t[:, a, c].rearrange("p r w -> p (r w)")[:, window],
                                   lambda t, a: t[:, h % 2, a, :], start=(r == 0),
                                   stop=(r == HEADS_PER_CHUNK - 1),
                                   low=(probsT_lo_made, from_one(head)))
                    last.then_inc(mixed, 1)
                if name == "spread":
                    pe.wait_ge(inverse_wide_made, batch)
                    pe.wait_ge(probsT_hi_made, from_one(nth(j, H, HEADS * b + HEADS - 1)))
                    pe.wait_ge(probsT_lo_made, from_one(nth(j, H, HEADS * b + HEADS - 1)))
                    if b + 1 < PAIR:
                        pe.wait_ge(k_made, nth(j, PAIR, b + 1))
                    for c in range(C):
                        for n in range(C):
                            last = nc.tensor.matmul(
                                turn_bank[:, c * N + n * P:c * N + (n + 1) * P],
                                inverse_wide[:, n].rearrange("p h d -> p (h d)")[:, c * P:(c + 1) * P],
                                ident[:], is_transpose=True, start=True, stop=True)
                    last.then_inc(spread, 1)
                if name == "o":
                    pe.wait_ge(oT_hi_made, batch)
                    for n in range(C):
                        last = product(mix_bank[:, n * D:(n + 1) * D], (oT_hi, oT_lo), w_s["wo"],
                                       columns(n), whole, late=0, low=(oT_lo_made, batch))
                    last.then_inc(o_prod, 1)

            plan = TENSOR_ORDER

            def body(i, j):
                for name, a, b in plan:
                    if name in "uarzvwt":
                        if i is not None:
                            gated(name, a, b, i)
                    elif j is not None:
                        attention(name, a, b, j, stacked=i is not None)

            nc.tensor.nop().then_inc(mixed, 1)
            pe.wait_ge(ident_ready, 1)
            iterations(pe, body)

        @block.scalar
        def _(act):
            def copy(to, source, done):
                nc.scalar.activation(to, source, ACT.Identity).then_inc(done, 1)

            def split_x(i):
                act.wait_ge(x_loaded, nth(i, 2 * PAIR, 2 * PAIR - 1) * 16)
                wait_ge(act, a_prod, nth(i, G, -1))
                for c in range(C):
                    copy(hT_hi[:, c, :], xT_in[:, c, :], hT_hi_made)
                for c in range(C):
                    copy(h_hi[:, c, :], x_in[:, c, :], h_hi_made)

            def prepare(which):
                for n in which:
                    name = all_weights[n][1]
                    if name in CHANGED:
                        act.wait_ge(sum_ready, CHANGED.index(name) + 1)
                    else:
                        act.wait_ge(stage_loaded[n % 3], 16 * (n // 3 + 1))
                    copy(flat(w_s[name][0]), stage[n % 3][:, 0:C, :].rearrange("p c n -> p (c n)"), hi_ready)

            for made in (probs_made, probsT_hi_made, spread_copied):
                nc.scalar.nop().then_inc(made, 1)
            split_x(0)
            prepare(SETUP)
            act.wait_ge(bias_ready, 1)

            plan = SCALAR_ORDER

            def gated(name, s, c, i):
                one = nth(i, G, C * s + c)
                if name == "u_copy":
                    act.wait_ge(u_prod, one)
                    wait_ge(act, z_summed, lately(i, G, C * (s - 1) + c))
                    copy(uT[:, c, :], gate_bank[c][:], u_copied)
                if name == "a_hi":
                    act.wait_ge(a_prod, one)
                    copy(aT_hi[:, c, :], gate_bank[2 + c][:], a_hi_made)
                if name == "r_tanh":
                    act.wait_ge(r_summed, one)
                    nc.scalar.activation(r_tanh[:, c, :], r_tanh[:, c, :], ACT.Tanh,
                                         bias=bias_r[:, c:c + 1], scale=0.5).then_inc(r_tanh_made, 1)
                if name == "rh_hi":
                    act.wait_ge(rh_made, one)
                    copy(rhT_hi[:, c, :], rhT[:, c, :], rh_hi_made)
                if name == "z_tanh":
                    act.wait_ge(z_summed, one)
                    wait_ge(act, keep_made, lately(i, G, C * (s - 1) + c))
                    nc.scalar.activation(z_tanh[:, c, :], z_tanh[:, c, :], ACT.Tanh,
                                         bias=bias_z[:, c:c + 1], scale=0.5).then_inc(z_tanh_made, 1)
                if name == "cand":
                    act.wait_ge(v_prod, one)
                    nc.scalar.activation(cand[:, c, :], gate_bank[c][:], ACT.Tanh,
                                         bias=bias_v[:, c:c + 1]).then_inc(cand_made, 1)
                if name == "hT_hi":
                    act.wait_ge(h_new, one)
                    copy(hT_hi[:, c, :], hT[:, c, :], hT_hi_made)
                if name == "h_hi":
                    act.wait_ge(h_turned, nth(i, STEPS, s))
                    for n in range(C):
                        copy(h_hi[:, n, :], gate_bank[2 + n][:], h_hi_made)
                if name == "split_x":
                    split_x(i + 1)

            def attention(name, b, h, j):
                batch, head = nth(j, PAIR, b), nth(j, H, HEADS * b + h)
                if name == "x1T_hi":
                    act.wait_ge(x1_turned, batch)
                    copy(flat(x1T_hi), score_bank[0][:], x1T_hi_made)
                if name == "q":
                    act.wait_ge(q_prod, batch)
                    for c in range(C):
                        last = nc.scalar.activation(qT[:, c, :], score_bank[1][:, c * N:(c + 1) * N],
                                                    ACT.Identity, bias=bias_q[:, c:c + 1],
                                                    scale=-SCORE_SCALE)
                    last.then_inc(q_made, 1)
                    act.wait_ge(q_made, batch)
                    copy(flat(qT_s[0]), flat(qT), q_hi_made)
                if name == "k":
                    act.wait_ge(k_prod, batch)
                    for c in range(C):
                        last = nc.scalar.activation(kT[:, c, :], turn_bank[:, c * N:(c + 1) * N],
                                                    ACT.Identity, bias=raw_bias[:, 6, c:c + 1])
                    last.then_inc(k_made, 1)
                    act.wait_ge(k_made, batch)
                    copy(flat(kT_s[0]), flat(kT), k_hi_made)
                if name == "v_hi":
                    act.wait_ge(v_made, batch)
                    act.wait_ge(pads_zero, 2)
                    copy(windows(v_s[0]), by_head(v_sb), v_hi_made)
                if name == "exp":
                    for n in range(C):
                        act.wait_ge(masked, from_one(nth(j, HC, (HEADS * b + h) * C + n)))
                        nc.scalar.activation(
                            probs[:, h % 2, n, :], neg_scores[:, h % 2, n, :], ACT.Exp, scale=-1.0,
                            bias=neg_max[b][:, h, n:n + 1],
                            accum_out=sums[b][:, h, n:n + 1]).then_inc(probs_made, 1)
                if name == "probsT_hi":
                    act.wait_ge(probs_turned, head)
                    act.wait_ge(mixed, from_one(lately(j, H, HEADS * b + h - 2)))
                    copy(probsT_s[0][:, h % 2].rearrange("p c n -> p (c n)"), turn_bank[:], probsT_hi_made)
                if name == "spread":
                    act.wait_ge(spread, batch)
                    copy(flat(spread_sb), turn_bank[:], spread_copied)
                if name == "oT_hi":
                    act.wait_ge(oT_made, batch)
                    copy(flat(oT_hi), flat(oT), oT_hi_made)

            GATED = ("u_copy", "a_hi", "r_tanh", "rh_hi", "z_tanh", "cand", "hT_hi", "h_hi", "split_x")

            def body(i, j):
                for name, a, b in plan:
                    if name in GATED:
                        if i is not None:
                            gated(name, a, b, i)
                            if j is None and name == "z_tanh" and b == C - 1:
                                prepare(AT_STEP.get(a, ()))
                    elif j is not None:
                        attention(name, a, b, j)

            iterations(act, body)

        @block.vector
        def _(dve):
            def rest(lo, full, hi, done):
                nc.vector.tensor_tensor(lo, full, hi.bitcast(f32), ALU.subtract).then_inc(done, 1)

            def split_x(i):
                for c in range(C):
                    dve.wait_ge(hT_hi_made, nth(i, G, c))
                    rest(hT_lo[:, c, :], xT_in[:, c, :], hT_hi[:, c, :], hT_lo_made)
                for c in range(C):
                    dve.wait_ge(h_hi_made, nth(i, G, c))
                    rest(h_lo[:, c, :], x_in[:, c, :], h_hi[:, c, :], h_lo_made)

            def prepare(which):
                for n in which:
                    _, name, chunks = all_weights[n]
                    st = stage[n % 3]
                    first = st[:, 0:C, :].rearrange("p c n -> p (c n)")
                    if name in CHANGED:
                        dve.wait_ge(stage_loaded[n % 3], 16 * (n // 3 + 1))
                        if chunks > C:
                            nc.vector.tensor_tensor(first, first, st[:, C:2 * C, :].rearrange("p c n -> p (c n)"),
                                                    ALU.add).then_inc(sum_ready, 1)
                        else:
                            nc.vector.tensor_scalar(first, first, 0.5, None, ALU.mult).then_inc(sum_ready, 1)
                    dve.wait_ge(hi_ready, n + 1)
                    nc.vector.tensor_tensor(flat(w_s[name][1]), first, flat(w_s[name][0]).bitcast(f32),
                                            ALU.subtract).then_inc(lo_ready, 1)

            for made in (masked, probsT_lo_made, y2_made):
                nc.vector.nop().then_inc(made, 1)
            nc.vector.memset(power[:], -0.5)
            split_x(0)
            prepare(SETUP)
            dve.wait_ge(small_loaded, 16 * SMALL)
            nc.vector.tensor_tensor(bias_r[:], raw_bias[:, 1, :], raw_bias[:, 3, :], ALU.add)
            nc.vector.tensor_tensor(bias_z[:], raw_bias[:, 0, :], raw_bias[:, 3, :], ALU.add)
            nc.vector.tensor_tensor(bias_v[:], raw_bias[:, 2, :], raw_bias[:, 4, :], ALU.add)
            nc.vector.tensor_scalar(flat(mask), flat(mask), -1.0, 1.0, ALU.mult, ALU.add).then_inc(bias_step, 1)
            dve.wait_ge(bias_step, 1)
            nc.vector.tensor_scalar(flat(mask), flat(mask), MASK, None, ALU.mult)
            nc.vector.tensor_scalar(bias_r[:], bias_r[:], 0.5, None, ALU.mult)
            nc.vector.tensor_scalar(bias_z[:], bias_z[:], 0.5, None, ALU.mult)
            nc.vector.tensor_scalar(bias_q[:], raw_bias[:, 5, :], -SCORE_SCALE, None,
                                    ALU.mult).then_inc(bias_ready, 1)

            plan = VECTOR_ORDER

            def gated(name, s, c, i):
                one = nth(i, G, C * s + c)

                def h_old():
                    return hT[:, c, :] if s else xT_in[:, c, :]

                if name == "a_lo":
                    dve.wait_ge(a_hi_made, one)
                    rest(aT_lo[:, c, :], gate_bank[2 + c][:], aT_hi[:, c, :], a_lo_made)
                if name == "r_sum":
                    dve.wait_ge(r_prod, one)
                    dve.wait_ge(u_copied, one)
                    nc.vector.tensor_tensor(r_tanh[:, c, :], gate_bank[c][:], uT[:, c, :],
                                            ALU.add).then_inc(r_summed, 1)
                if name == "rh":
                    dve.wait_ge(r_tanh_made, one)
                    wait_ge(dve, rh_lo_made, lately(i, G, C * (s - 1) + c))
                    nc.vector.scalar_tensor_tensor(out=rhT[:, c, :], in0=r_tanh[:, c, :], scalar=1.0,
                                                   in1=h_old(), op0=ALU.add,
                                                   op1=ALU.mult).then_inc(rh_made, 1)
                if name == "z_sum":
                    dve.wait_ge(z_prod, one)
                    nc.vector.tensor_tensor(z_tanh[:, c, :], gate_bank[2 + c][:], uT[:, c, :],
                                            ALU.add).then_inc(z_summed, 1)
                if name == "gate":
                    dve.wait_ge(rh_made, one)
                    dve.wait_ge(z_tanh_made, one)
                    nc.vector.tensor_scalar(gate[:, c, :], z_tanh[:, c, :], 0.5, 0.5, ALU.mult,
                                            ALU.add).then_inc(gate_made, 1)
                if name == "move":
                    dve.wait_ge(gate_made, one)
                    dve.wait_ge(cand_made, one)
                    nc.vector.tensor_tensor(cand[:, c, :], gate[:, c, :], cand[:, c, :],
                                            ALU.mult).then_inc(move_made, 1)
                if name == "h_new":
                    dve.wait_ge(kept_made, one)
                    dve.wait_ge(move_made, one)
                    nc.vector.tensor_tensor(hT[:, c, :], kept[:, c, :], cand[:, c, :],
                                            ALU.add).then_inc(h_new, 1)
                if name == "hT_lo":
                    dve.wait_ge(hT_hi_made, nth(i, G, C * (s + 1) + c))
                    rest(hT_lo[:, c, :], hT[:, c, :], hT_hi[:, c, :], hT_lo_made)
                if name == "h_lo":
                    for n in range(C):
                        dve.wait_ge(h_hi_made, nth(i, G, C * (s + 1) + n))
                        rest(h_lo[:, n, :], gate_bank[2 + n][:], h_hi[:, n, :], h_lo_made)
                if name == "split_x":
                    split_x(i + 1)
                if name == "y1":
                    dve.wait_ge(h_turned, nth(i, STEPS, s))
                    dve.wait_ge(x_kept, nth(i, 1, 0))
                    for n in range(C):
                        nc.vector.tensor_tensor(y1[:, n].rearrange("p b n -> p (b n)"), gate_bank[2 + n][:],
                                                y1[:, n].rearrange("p b n -> p (b n)"),
                                                ALU.add).then_inc(y1_made, 1)
                    dve.wait_ge(y1_made, nth(i, C, C - 1))
                    for n in range(C):
                        for b in range(PAIR):
                            last = nc.vector.bn_stats(stats1[:, n * PAIR + b, :], y1[:, n, b, :])
                    last.then_inc(stats1_made, 1)
                    dve.wait_ge(stats1_made, nth(i, 1, 0))
                    stand_alone(dve)
                    for g in range(C * PAIR):
                        last = nc.vector.bn_aggr(mv1[:, g, :], stats1[:, g, :])
                    last.then_inc(mv1_made, 1)
                    dve.wait_ge(mv1_made, nth(i, 1, 0))
                    nc.vector.tensor_scalar(var1[:], mv1[:, :, 1], EPS, None, ALU.add).then_inc(var1_made, 1)
                if name == "norm1":
                    dve.wait_ge(rstd1_made, nth(i, 1, 0))
                    for n in range(C):
                        for b in range(PAIR):
                            g = n * PAIR + b
                            last = nc.vector.tensor_scalar(x1[:, n, b, :], y1[:, n, b, :], mv1[:, g, 0:1],
                                                           rstd1[:, g:g + 1], ALU.subtract, ALU.mult)
                    last.then_inc(x1_made, 1)

            def attention(name, b, h, j):
                batch, head = nth(j, PAIR, b), nth(j, H, HEADS * b + h)
                if name == "x1T_lo":
                    dve.wait_ge(x1T_hi_made, batch)
                    rest(flat(x1T_lo), score_bank[0][:], flat(x1T_hi), x1T_lo_made)
                if name == "q_lo":
                    dve.wait_ge(q_hi_made, batch)
                    rest(flat(qT_s[1]), flat(qT), flat(qT_s[0]), q_lo_made)
                if name == "k_lo":
                    dve.wait_ge(k_hi_made, batch)
                    rest(flat(kT_s[1]), flat(kT), flat(kT_s[0]), k_lo_made)
                if name == "v":
                    dve.wait_ge(v_out, batch)
                    nc.vector.tensor_tensor(v_sb[:], score_bank[0][:].rearrange("p (c n) -> p c n", c=C),
                                            bv_rows[:].unsqueeze(1).to_broadcast([P, C, D]),
                                            ALU.add).then_inc(v_made, 1)
                if name == "v_lo":
                    dve.wait_ge(v_hi_made, batch)
                    dve.wait_ge(pads_zero, 2)
                    rest(windows(v_s[1]), by_head(v_sb), windows(v_s[0]), v_lo_made)
                if name == "mask":
                    dve.wait_ge(scored, head)
                    dve.wait_ge(probs_made, from_one(lately(j, HC, (HEADS * b + h - 1) * C - 1)))
                    stand_alone(dve)
                    for n in range(C):
                        nc.vector.tensor_tensor_reduce(
                            out=neg_scores[:, h % 2, n, :], in0=score_bank[h % 2][:, n * N:(n + 1) * N],
                            in1=mask[:, n, :], scale=1.0, scalar=3.4e38, op0=ALU.add, op1=ALU.min,
                            accum_out=neg_max[b][:, h, n:n + 1]).then_inc(masked, 1)
                if name == "probsT_lo":
                    dve.wait_ge(probsT_hi_made, from_one(head))
                    rest(probsT_s[1][:, h % 2].rearrange("p c n -> p (c n)"), turn_bank[:],
                         probsT_s[0][:, h % 2].rearrange("p c n -> p (c n)"), probsT_lo_made)
                if name == "inverse":
                    dve.wait_ge(probs_made, from_one(nth(j, HC, (HEADS * b + h + 1) * C - 1)))
                    nc.vector.reciprocal(inverse[b][:], sums[b][:]).then_inc(inverse_made, 1)
                    dve.wait_ge(inverse_made, batch)
                    for n in range(C):
                        last = nc.vector.tensor_copy(
                            inverse_wide[:, n], inverse[b][:, :, n:n + 1].to_broadcast([P, HEADS, HEAD_DIM]))
                    last.then_inc(inverse_wide_made, 1)
                if name == "oT":
                    dve.wait_ge(spread_copied, from_one(batch))
                    dve.wait_ge(mixed, from_one(nth(j, H, HEADS * b + HEADS - 1)))
                    nc.vector.tensor_tensor(flat(oT), mix_bank[:], flat(spread_sb),
                                            ALU.mult).then_inc(oT_made, 1)
                if name == "oT_lo":
                    dve.wait_ge(oT_hi_made, batch)
                    rest(flat(oT_lo), flat(oT), flat(oT_hi), oT_lo_made)
                if name == "y2":
                    dve.wait_ge(o_prod, batch)
                    dve.wait_ge(x1_bo_made, batch)
                    dve.wait_ge(stored[b], from_one(j) * 16)
                    nc.vector.tensor_tensor(flat(y2[b]), mix_bank[:], flat(x1_bo[b]),
                                            ALU.add).then_inc(y2_made, 1)
                    dve.wait_ge(y2_made, from_one(batch))
                    for n in range(C):
                        last = nc.vector.bn_stats(stats2[b][:, n, :], y2[b][:, n, :])
                    last.then_inc(stats2_made, 1)
                    dve.wait_ge(stats2_made, batch)
                    stand_alone(dve)
                    for n in range(C):
                        last = nc.vector.bn_aggr(mv2[b][:, n, :], stats2[b][:, n, :])
                    last.then_inc(mv2_made, 1)
                    dve.wait_ge(mv2_made, batch)
                    nc.vector.tensor_scalar(var2[b][:], mv2[b][:, :, 1], EPS, None,
                                            ALU.add).then_inc(var2_made, 1)
                if name == "norm2":
                    dve.wait_ge(rstd2_made, batch)
                    for n in range(C):
                        last = nc.vector.tensor_scalar(y2[b][:, n, :], y2[b][:, n, :],
                                                       mv2[b][:, n, 0:1], rstd2[b][:, n:n + 1],
                                                       ALU.subtract, ALU.mult)
                    last.then_inc(out_made, 1)

            GATED = ("a_lo", "r_sum", "rh", "z_sum", "gate", "move", "h_new", "hT_lo", "h_lo", "split_x",
                     "y1", "norm1")

            def body(i, j):
                for name, a, b in plan:
                    if name in GATED:
                        if i is not None:
                            gated(name, a, b, i)
                            if j is None and name == "gate" and b == C - 1:
                                prepare(AT_STEP.get(a, ()))
                    elif j is not None:
                        attention(name, a, b, j)

            iterations(dve, body)

        @block.gpsimd
        def _(pool):
            nc.gpsimd.memset(ident[:], 0.0).then_inc(ident_zero, 1)
            pool.wait_ge(ident_zero, 1)
            nc.gpsimd.affine_select(out=ident[:], in_=ident[:], compare_op=ALU.not_equal, fill=1.0, base=0,
                                    pattern=[[-1, P]], channel_multiplier=1).then_inc(ident_ready, 1)
            for part in v_s:
                nc.gpsimd.memset(part[:].bitcast(f32), 0.0).then_inc(pads_zero, 1)
            pool.wait_ge(small_loaded, 16 * SMALL)

            plan = POOL_ORDER

            def gated(name, s, c, i):
                one = nth(i, G, C * s + c)
                if name == "keep_x":
                    pool.wait_ge(x_loaded, nth(i, 2 * PAIR, 2 * PAIR - 1) * 16)
                    wait_ge(pool, x1_made, nth(i, 1, -1))
                    stand_alone(pool)
                    nc.gpsimd.tensor_copy(y1[:].rearrange("p c b n -> p c (b n)"), x_in[:]).then_inc(x_kept, 1)
                if name == "rh_lo":
                    pool.wait_ge(rh_hi_made, one)
                    nc.gpsimd.tensor_tensor(rhT_lo[:, c, :], rhT[:, c, :], rhT_hi[:, c, :].bitcast(f32),
                                            ALU.subtract).then_inc(rh_lo_made, 1)
                if name == "keep":
                    pool.wait_ge(z_tanh_made, one)
                    wait_ge(pool, h_new, lately(i, G, C * (s - 1) + c))
                    stand_alone(pool)
                    nc.gpsimd.tensor_scalar(kept[:, c, :], z_tanh[:, c, :], -0.5, 0.5, ALU.mult,
                                            ALU.add).then_inc(keep_made, 1)
                    pool.wait_ge(keep_made, one)
                    nc.gpsimd.tensor_tensor(kept[:, c, :], kept[:, c, :],
                                            hT[:, c, :] if s else xT_in[:, c, :],
                                            ALU.mult).then_inc(kept_made, 1)
                if name == "norm1":
                    pool.wait_ge(var1_made, nth(i, 1, 0))
                    nc.gpsimd.tensor_tensor(rstd1[:], var1[:], power[:], ALU.pow).then_inc(rstd1_made, 1)

            def attention(name, b, j):
                batch = nth(j, PAIR, b)
                if name == "x1_bo":
                    pool.wait_ge(x1_made, nth(j, 1, 0))
                    pool.wait_ge(y2_made, from_one(nth(j, PAIR, -1)))
                    nc.gpsimd.tensor_tensor(x1_bo[b][:], x1[:, :, b, :],
                                            bo_rows[:].unsqueeze(1).to_broadcast([P, C, D]),
                                            ALU.add).then_inc(x1_bo_made, 1)
                if name == "norm2":
                    pool.wait_ge(var2_made, batch)
                    nc.gpsimd.tensor_tensor(rstd2[b][:], var2[b][:], power[:, 0:C],
                                            ALU.pow).then_inc(rstd2_made, 1)

            def body(i, j):
                for name, a, b in plan:
                    if name in ("keep_x", "rh_lo", "keep", "norm1"):
                        if i is not None:
                            gated(name, a, b, i)
                    elif j is not None:
                        attention(name, a, j)

            iterations(pool, body)


def kernel(**inputs):
    import numpy as np
    import concourse.bacc as bacc
    from concourse import mybir as mb
    from concourse.bass_utils import run_bass_kernel_spmd

    def turned(a):
        return np.ascontiguousarray(np.swapaxes(a, -1, -2))

    g0, g1 = "L0_gnn_", "L1_gnn_"
    arrays = {"x": inputs["x"], "xT": turned(inputs["x"]), "adj": inputs["adj"], "adjT": turned(inputs["adj"])}
    for n in ("w3", "u3", "w4", "w5", "u5"):
        arrays[n + "T"] = turned(inputs[f"{g0}{n}_w"])
        arrays[n + "b"] = inputs[f"{g0}{n}_b"]
    for n in "qkvo":
        arrays["w" + n] = inputs[f"{g1}W{n}"]
        arrays["b" + n] = inputs[f"{g1}b{n}"]
    for n in ("w3b", "w4b", "w5b", "u3b", "u5b", "bq", "bk"):
        arrays[n] = turned(arrays[n].reshape(C, P))
    arrays = {n: np.ascontiguousarray(a) for n, a in arrays.items()}

    nc = bacc.Bacc("TRN2", target_bir_lowering=False, num_devices=1)
    args = {n: nc.dram_tensor(n, a.shape, mb.dt.from_np(a.dtype), kind="ExternalInput").ap()
            for n, a in arrays.items()}
    out = nc.dram_tensor("out", arrays["x"].shape, mb.dt.float32, kind="ExternalOutput").ap()
    build(nc, out=out, **args)
    return run_bass_kernel_spmd(nc, [arrays], core_ids=[0]).results[0]["out"]
```
